# Optimizing a Trainium2 kernel written in Bass

```python
import numpy as np
import jax
import jax.numpy as jnp

def _softmax(x, axis=-1):
    return jax.nn.softmax(x, axis=axis)
def _gelu(x):
    return jax.nn.gelu(x, approximate=True)
def _silu(x):
    return jax.nn.silu(x)
def _sigmoid(x):
    return jax.nn.sigmoid(x)
def _layernorm(x, axis=-1, eps=1e-5):
    m = jnp.mean(x, axis=axis, keepdims=True)
    v = jnp.var(x, axis=axis, keepdims=True)
    return (x - m) / jnp.sqrt(v + eps)
def _scatter_add(tgt, idx, src, axis=0):
    return tgt.at[idx].add(src)
def _segment_sum(src, seg, n):
    return jax.ops.segment_sum(src, seg, n)

kernel_name = 'mk_adj_resnorm_d2_adj_256_1ca573'

def setup_inputs(seed: int = 0):
    np.random.seed(seed)
    _w = jnp.asarray
    def _rec_inputs():
        import jax
        import jax.numpy as jnp
        _gk = jax.random.key(seed)
        x = -0.0002928 + 1 * jax.random.normal(jax.random.fold_in(_gk, 1), (8, 2048, 256), jnp.float32)
        _a = jax.random.bernoulli(jax.random.fold_in(_gk, 2), 0.0078125, (8, 2048, 2048))
        _a = jnp.logical_or(_a, jnp.swapaxes(_a, -1, -2))
        _a = jnp.logical_or(_a, jnp.eye(2048, dtype=bool))
        _af = _a.astype(jnp.float32)
        _af = _af * jax.random.uniform(jax.random.fold_in(_gk, 3), (8, 2048, 2048), jnp.float32, 0.05, 1)
        adj = _af
        return x, adj
    x, adj = _rec_inputs()
    def _L0_gnn_setup():
        import jax, jax.numpy as jnp
        import numpy as np
        B, N, C_IN, C_OUT = (8, 2048, 256, 256)
        key = jax.random.key(seed)
        k1, k2, k3 = jax.random.split(key, 3)
        x = jax.random.normal(k1, (B, N, C_IN), dtype=jnp.float32)
        adj = jax.random.uniform(k2, (B, N, N), dtype=jnp.float32)
        limit = float(np.sqrt(6.0 / (C_IN + C_OUT)))
        weight = jax.random.uniform(k3, (C_IN, C_OUT), minval=-limit, maxval=limit, dtype=jnp.float32)
        bias = jnp.zeros((C_OUT,), dtype=jnp.float32)
        return {'x': x, 'adj': adj, 'weight': weight, 'bias': bias}
    _L0_gnn_all = _L0_gnn_setup()
    _L0_gnn_in = {k: v for k, v in _L0_gnn_all.items() if k in ('weight', 'bias', )}
    del _L0_gnn_all

    def _L1_gnn_setup():
        import jax, jax.numpy as jnp
        import numpy as np
        B, N, D, H = (8, 2048, 256, 1024)
        RMS_EPS = 1e-06

        def _rmsnorm(h, w, eps=RMS_EPS):
            var = jnp.mean(jnp.square(h), axis=-1, keepdims=True)
            return h * jax.lax.rsqrt(var + eps) * w
        key = jax.random.key(seed)
        ks = jax.random.split(key, 5)
        x = jax.random.normal(ks[0], (B, N, D), dtype=jnp.float32)
        adjacency = jax.random.uniform(ks[1], (B, N, N), dtype=jnp.float32)
        epsilon = jnp.zeros((), dtype=jnp.float32)
        W1 = jax.random.normal(ks[2], (D, H), dtype=jnp.float32) * (1.0 / np.sqrt(D))
        b1 = jnp.zeros((H,), dtype=jnp.float32)
        rms_weight = jnp.ones((H,), dtype=jnp.float32)
        W2 = jax.random.normal(ks[3], (H, D), dtype=jnp.float32) * (1.0 / np.sqrt(H))
        b2 = jnp.zeros((D,), dtype=jnp.float32)
        return {'x': x, 'adjacency': adjacency, 'epsilon': epsilon, 'W1': W1, 'b1': b1, 'rms_weight': rms_weight, 'W2': W2, 'b2': b2}
    _L1_gnn_all = _L1_gnn_setup()
    _L1_gnn_in = {k: v for k, v in _L1_gnn_all.items() if k in ('epsilon', 'W1', 'b1', 'rms_weight', 'W2', 'b2', )}
    del _L1_gnn_all

    return {
        "x": x,
        "adj": adj,
        "L0_gnn_weight": _L0_gnn_in["weight"],
        "L0_gnn_bias": _L0_gnn_in["bias"],
        "L1_gnn_epsilon": _L1_gnn_in["epsilon"],
        "L1_gnn_W1": _L1_gnn_in["W1"],
        "L1_gnn_b1": _L1_gnn_in["b1"],
        "L1_gnn_rms_weight": _L1_gnn_in["rms_weight"],
        "L1_gnn_W2": _L1_gnn_in["W2"],
        "L1_gnn_b2": _L1_gnn_in["b2"],
    }

def reference(x, adj, L0_gnn_weight, L0_gnn_bias, L1_gnn_epsilon, L1_gnn_W1, L1_gnn_b1, L1_gnn_rms_weight, L1_gnn_W2, L1_gnn_b2):
    import jax
    import jax.numpy as jnp
    def _L0_gnn_ref(x, adj, weight, bias):
        import jax, jax.numpy as jnp
        import numpy as np
        B, N, C_IN, C_OUT = (8, 2048, 256, 256)
        d_inv_sqrt = (jnp.sum(adj, axis=-1) + 1e-05) ** (-0.5)
        adj_norm = d_inv_sqrt[..., :, None] * adj * d_inv_sqrt[..., None, :]
        support = jnp.einsum('bni,io->bno', x, weight)
        return jnp.einsum('bnm,bmo->bno', adj_norm, support) + bias

    def _L1_gnn_ref(x, adjacency, epsilon, W1, b1, rms_weight, W2, b2):
        import jax, jax.numpy as jnp
        import numpy as np
        B, N, D, H = (8, 2048, 256, 1024)
        RMS_EPS = 1e-06

        def _rmsnorm(h, w, eps=RMS_EPS):
            var = jnp.mean(jnp.square(h), axis=-1, keepdims=True)
            return h * jax.lax.rsqrt(var + eps) * w
        neighbor_sum = jnp.einsum('bnm,bmd->bnd', adjacency, x)
        agg = epsilon * x + neighbor_sum
        h = jnp.einsum('bnd,dh->bnh', agg, W1) + b1
        h = jax.nn.silu(_rmsnorm(h, rms_weight))
        out = jnp.einsum('bnh,hd->bnd', h, W2) + b2
        return out

    x = _layernorm(x + _L0_gnn_ref(x, adj, L0_gnn_weight, L0_gnn_bias), axis=-1)
    x = _layernorm(x + _L1_gnn_ref(x, adj, L1_gnn_epsilon, L1_gnn_W1, L1_gnn_b1, L1_gnn_rms_weight, L1_gnn_W2, L1_gnn_b2), axis=-1)
    return x


_drawn_inputs = setup_inputs


def setup_inputs(seed=0):
    import zlib

    import numpy as np

    out = dict(_drawn_inputs(seed))
    spreads = {'L0_gnn_bias': (0.0, 0.1),
     'L1_gnn_b1': (0.0, 0.558),
     'L1_gnn_rms_weight': (1.0, 0.2),
     'L1_gnn_b2': (0.0, 0.1)}
    factors = {}
    for name, (base, spread) in spreads.items():
        noise = np.random.default_rng([zlib.crc32(name.encode()), seed]).standard_normal(out[name].shape)
        drawn = base * np.exp(spread * noise) if base else spread * noise
        out[name] = jnp.asarray(drawn.astype(out[name].dtype))
    for name, factor in factors.items():
        out[name] = (out[name] * factor).astype(out[name].dtype)
    return out
```

```python
from contextlib import ExitStack

import concourse.bass as bass
from concourse import mybir

F32 = mybir.dt.float32
F32R = mybir.dt.float32r
ALU = mybir.AluOpType
ACT = mybir.ActivationFunctionType
P = 128
QUADS = 4
QP = P // QUADS
LN_EPS = 1e-5
DEG_EPS = 1e-5
RMS_EPS = 1e-6


def build(nc, x, adj, w0, bias0, eps, w1, b1, rms_w, w2, b2, y):
    B, N, D = x.shape
    H = w1.shape[1]
    NT = N // P
    CH = 512
    NJ = N // CH
    TPC = CH // P
    DK = D // P
    HK = H // P
    QW = N // QUADS
    UT = 2
    UPC = NT // UT
    UNITS = 2 * NJ * UPC
    RING = 3
    assert D == 256 and QW == CH and UPC == 8 and TPC == QUADS and DK == 2

    adj_rows = adj.rearrange("b (Q k a) (q f) -> b k Q q a f", Q=QUADS, a=QP, q=QUADS)
    x_rows = x.rearrange("b (q t c) d -> b t q c d", q=QUADS, c=QP)
    y_rows = y.rearrange("b (q t c) d -> b t q c d", q=QUADS, c=QP)
    agg_scratch = nc.dram_tensor("agg_scratch", [B * NJ, P, 2 * DK * CH], F32)
    x1_scratch = nc.dram_tensor("x1_scratch", [B * NJ, P, TPC * D], F32)

    with ExitStack() as both:
        def keep(name, shape, dt=F32):
            return both.enter_context(nc.sbuf_tensor(name, shape, dt))

        ident = keep("ident", [P, P])
        psum = [both.enter_context(nc.psum_tensor(f"bank{i}", [P, CH], F32)) for i in range(8)]

        shared = locals()
        aggregate(nc, shared)
        dense(nc, shared)


def aggregate(nc, g):
    B, N, D, NT, CH, NJ, TPC, DK, UT, UPC, UNITS, RING = (
        g[k] for k in ("B", "N", "D", "NT", "CH", "NJ", "TPC", "DK", "UT", "UPC", "UNITS", "RING"))
    adj_rows, x_rows, agg_scratch, x1_scratch = (
        g[k] for k in ("adj_rows", "x_rows", "agg_scratch", "x1_scratch"))
    ident, psum = g["ident"], g["psum"]
    last_batch = B - 1
    CPB = 2 * NJ
    LU = NJ * UPC
    XS = 4

    with ExitStack() as ctx:
        def sb(name, shape, dt=F32):
            return ctx.enter_context(nc.sbuf_tensor(name, shape, dt))

        def sem(name):
            return ctx.enter_context(nc.semaphore(name))

        at = sb("at", [P, NT, N])
        feat = sb("feat", [P, NT, 2, D], F32R)
        stage = sb("stage", [P, 2, QUADS, CH])
        x1 = stage[:, :, :, :].rearrange("p s q f -> p (s q f)").rearrange("p (t d) -> p t d", d=D)
        unit_hi = sb("unit_hi", [P, RING, UT * CH], F32R)
        unit_lo = sb("unit_lo", [P, RING, UT * CH], F32R)
        agg = sb("agg", [P, 2, DK, CH], F32R)
        w0s = sb("w0s", [P, DK, 2, D], F32R)
        fold = sb("fold", [P, P])
        bias = sb("bias", [P, D])
        eps_sb = sb("eps_sb", [P, 1])
        x_in = sb("x_in", [P, XS, D])
        y_lo = sb("y_lo", [P, 2, D])
        part = sb("part", [P, NT, QUADS])
        deg = sb("deg", [P, NT])
        dinv = sb("dinv", [P, NT])
        minus_half = sb("minus_half", [P, NT])
        wait_here = sb("wait_here", [P, 1])
        ln_eps = sb("ln_eps", [P, TPC])
        stats = sb("stats", [P, 6])
        mean_var = sb("mean_var", [P, TPC, 2])
        var_eps = sb("var_eps", [P, TPC])
        rstd = sb("rstd", [P, TPC])
        w0_in = x_in[:, 0:DK, :]

        agg_ps = [[psum[2 * s + ob] for ob in range(DK)] for s in range(2)]
        y_ps = psum[4:8]
        fold_ps = psum[7]

        rows_in = [sem(f"rows_in{s}") for s in range(2)]
        x_loaded = [sem(f"x_loaded{s}") for s in range(XS)]
        consts_in = sem("consts_in")
        pool_consts = sem("pool_consts")
        w0_hi = sem("w0_hi")
        w0_ready = sem("w0_ready")
        rows_summed = sem("rows_summed")
        transposed = sem("transposed")
        sums_folded = sem("sums_folded")
        deg_ready = sem("deg_ready")
        dinv_ready = sem("dinv_ready")
        hi_ready = sem("hi_ready")
        lo_ready = sem("lo_ready")
        unit_free = sem("unit_free")
        feat_hi = sem("feat_hi")
        feat_lo = sem("feat_lo")
        agg_hi = sem("agg_hi")
        agg_lo = sem("agg_lo")
        agg_stored = sem("agg_stored")
        y_ready = sem("y_ready")
        ylo_ready = sem("ylo_ready")
        y_used = sem("y_used")
        biased = sem("biased")
        summed = sem("summed")
        stats_done = sem("stats_done")
        var_ready = sem("var_ready")
        veps_ready = sem("veps_ready")
        rstd_ready = sem("rstd_ready")
        x1_ready = sem("x1_ready")
        x1_stored = sem("x1_stored")
        eps_added = sem("eps_added")
        block = ctx.enter_context(nc.Block())

        def over_batches(eng, body):
            with eng.Fori(0, last_batch) as b:
                body(b, False)
            body(last_batch, True)

        def slot_of(layer, j, u):
            return (j * UPC + u) % RING

        def units_before(layer, j, u):
            v = j * UPC + u
            if v >= RING:
                return layer * LU + v - RING + 1
            before = max(w for w in range(LU) if w % RING == v % RING) + 1
            return layer * LU - LU + before

        def at_unit(layer, j, u):
            return at[:, UT * u:UT * u + UT, j * CH:(j + 1) * CH]

        def ring_view(ring, layer, j, u):
            return ring[:, slot_of(layer, j, u), :].rearrange("p (t n) -> p t n", t=UT)

        def tiles_behind(j, u):
            return [TPC * (j - 1) + u // 2] if j >= 1 and u % 2 else []

        def feats_before(u):
            if u < 2:
                return []
            return list(range(0, UT * u + UT)) if u == 2 else list(range(UT * u, UT * u + UT))

        @block.sync
        def _(sp):
            sp.dma_start(w0_in, g["w0"].rearrange("(k p) d -> p k d", p=P)).then_inc(consts_in, 16)
            sp.dma_start(bias[:, :], g["bias0"].to_broadcast([P, D])).then_inc(consts_in, 16)
            sp.dma_start(eps_sb[:, :], g["eps"].to_broadcast([P, 1])).then_inc(consts_in, 16)

            def load_rows(b, k, sums):
                if sums is not None:
                    sp.wait_ge(rows_summed, sums)
                    sp.wait_ge(transposed, sums)
                for q in range(QUADS):
                    dst = stage[:, k % 2, q, :]
                    sp.dma_start(dst, adj_rows[b, k, q]).then_inc(rows_in[k % 2], 16)

            def load_x(b, t, residual):
                if residual and t < XS:
                    sp.wait_ge(feat_lo, b * 2 * NT + NT - XS + t + 1)
                elif residual:
                    sp.wait_ge(summed, b * NT + t - XS + 2)
                elif t < XS:
                    sp.wait_ge(summed, b * NT + 1)
                else:
                    sp.wait_ge(feat_lo, b * 2 * NT + t - XS + 1)
                dst = x_in[:, t % XS, :]
                sp.dma_start(dst, x_rows[b, t]).then_inc(x_loaded[t % XS], 16)

            for k in range(NT):
                load_rows(0, k, k - 1 if k >= 2 else None)
            sp.wait_ge(w0_ready, 1)

            def body(b, is_last):
                for t in range(NT):
                    load_x(b, t, False)

                def store_x1(j):
                    sp.wait_ge(x1_ready, b * NT + TPC * (j + 1))
                    sp.dma_start(x1_scratch[b * NJ + j],
                                 x1[:, TPC * j:TPC * (j + 1), :].rearrange("p t d -> p (t d)")).then_inc(x1_stored, 16)

                for j in range(NJ):
                    for t in range(TPC * j, TPC * (j + 1)):
                        load_x(b, t, True)
                    if j:
                        store_x1(j - 1)
                store_x1(NJ - 1)
                if not is_last:
                    sp.wait_ge(x1_stored, (b * NJ + NJ) * 16)
                    sp.wait_ge(feat_lo, (b + 1) * 2 * NT)
                    for k in range(NT):
                        load_rows(b + 1, k, b * NT + NT + k - 1 if k >= 2 else None)

            over_batches(sp, body)
            sp.wait_ge(x1_stored, B * NJ * 16)

        @block.scalar
        def _(act):
            def sum_rows(b, k):
                act.wait_ge(rows_in[k % 2], (b * NT // 2 + k // 2 + 1) * 16 * QUADS)
                if not (isinstance(b, int) and b == 0 and k == 0):
                    act.wait_ge(rows_summed, b * NT + k)
                if k == 0:
                    act.wait_ge(y_used, b * NT + 2)
                for q in range(QUADS):
                    last = act.activation(y_ps[q][:, :], stage[:, k % 2, q, :], ACT.Copy, accum_out=part[:, k, q:q + 1])
                last.then_inc(rows_summed, 1)

            act.sem_inc(agg_stored, 16)
            act.wait_ge(consts_in, 48)
            act.copy(w0s[:, :, 0, :], w0_in).then_inc(w0_hi, 1)
            for k in range(NT):
                sum_rows(0, k)

            def body(b, is_last):
                def split_feat(layer, t):
                    if layer == 0:
                        act.wait_ge(x_loaded[t % XS], (b * 2 * NT // XS + t // XS + 1) * 16)
                        act.activation(feat[:, t, 0, :], x_in[:, t % XS, :], ACT.Copy,
                                       scale=dinv[:, t:t + 1]).then_inc(feat_hi, 1)
                    else:
                        act.wait_ge(x1_ready, b * NT + t + 1)
                        act.copy(feat[:, t, 0, :], x1[:, t, :]).then_inc(feat_hi, 1)

                def split_agg(c):
                    act.wait_ge(unit_free, b * UNITS + UPC * (c + 1) + RING)
                    if 1 <= c <= NJ:
                        act.wait_ge(y_ready, b * NT + TPC * c)
                    else:
                        act.wait_ge(agg_stored, (b * NJ + (c - NJ if c else 0) + 1) * 16)
                    for ob in range(DK):
                        last = act.copy(agg[:, 0, ob, :], agg_ps[c % 2][ob][:, :])
                    last.then_inc(agg_hi, 1)

                def store_agg(c):
                    act.wait_ge(agg_lo, b * CPB + c + 2)
                    act.dma_start(agg_scratch[b * NJ + (c - NJ)],
                                  agg[:, :, :, :].bitcast(F32).rearrange("p h k n -> p (h k n)")).then_inc(agg_stored, 16)

                def scale_y(t):
                    act.wait_ge(y_ready, b * NT + t + 1)
                    act.wait_ge(y_used, b * NT + t + 1)
                    act.activation(y_lo[:, t % 2, :], y_ps[t % TPC][:, D:2 * D], ACT.Copy,
                                   scale=dinv[:, t:t + 1]).then_inc(ylo_ready, 1)

                for layer in range(2):
                    for j in range(NJ):
                        c = layer * NJ + j
                        for u in range(UPC):
                            if c and u == 0 and layer:
                                act.wait_ge(eps_added, b * NT + TPC * (j + 1))
                            if j == 0 and u == 2:
                                if layer == 0:
                                    act.wait_ge(dinv_ready, b + 1)
                                act.wait_ge(unit_free, b * UNITS + layer * LU + RING)
                                for t in range(2):
                                    split_feat(layer, t)
                            if c and u == 2:
                                split_agg(c - 1)
                            if j == 0:
                                for t in feats_before(u):
                                    if t >= 2:
                                        split_feat(layer, t)
                            if c > NJ and u == 4:
                                store_agg(c - 1)
                            if layer == 0 and j and u >= 4:
                                scale_y(TPC * (j - 1) + u - 4)
                            if c == NJ and u == 4:
                                for i in range(TPC):
                                    scale_y(TPC * (NJ - 1) + i)
                            if layer and not is_last:
                                for k in tiles_behind(j, u):
                                    sum_rows(b + 1, k)
                            if layer == 0 and u == 0:
                                act.wait_ge(transposed, b * NT + TPC * (j + 1))
                            act.wait_ge(unit_free, b * UNITS + RING + units_before(layer, j, u))
                            act.copy(ring_view(unit_hi, layer, j, u), at_unit(layer, j, u)).then_inc(hi_ready, 1)
                if not is_last:
                    for k in range(NT - TPC, NT):
                        sum_rows(b + 1, k)
                split_agg(CPB - 1)
                store_agg(CPB - 1)

            over_batches(act, body)
            act.wait_ge(agg_stored, (B * NJ + 1) * 16)

        @block.gpsimd
        def _(pool):
            pool.memset(minus_half[:, :], -0.5)
            pool.memset(ln_eps[:, :], LN_EPS)
            pool.memset(fold[:, :], 0.0).then_inc(pool_consts, 1)
            pool.memset(ident[:, :], 0.0).then_inc(pool_consts, 1)
            pool.wait_ge(pool_consts, 2)
            pool.affine_select(out=ident[:, :], in_=ident[:, :], compare_op=ALU.not_equal, fill=1.0, base=0,
                               pattern=[[-1, P]], channel_multiplier=1).then_inc(pool_consts, 1)
            for n, s in enumerate(range(-(QUADS - 1), QUADS)):
                if n:
                    pool.wait_ge(pool_consts, 3 + n)
                pool.affine_select(out=fold[:, :], in_=fold[:, :], compare_op=ALU.not_equal, fill=1.0,
                                   base=-QP * s, pattern=[[-1, P]], channel_multiplier=1).then_inc(pool_consts, 1)
            pool.wait_ge(consts_in, 48)

            def body(b, is_last):
                pool.wait_ge(deg_ready, b + 1)
                pool.tensor_tensor(dinv[:, :], deg[:, :], minus_half[:, :], ALU.pow).then_inc(dinv_ready, 1)
                for j in range(NJ):
                    for i in range(TPC):
                        t = TPC * j + i
                        pool.wait_ge(x_loaded[t % XS], (b * 2 * NT // XS + NT // XS + t // XS + 1) * 16)
                        pool.tensor_tensor(x_in[:, t % XS, :], x_in[:, t % XS, :], bias[:, :], ALU.add)\
                            .then_inc(biased, 1)
                    pool.wait_ge(var_ready, b * NJ + j + 1)
                    pool.tensor_tensor(var_eps[:, :], mean_var[:, :, 1], ln_eps[:, :], ALU.add).then_inc(veps_ready, 1)
                    pool.wait_ge(veps_ready, b * NJ + j + 1)
                    pool.tensor_tensor(rstd[:, :], var_eps[:, :], minus_half[:, 0:TPC], ALU.pow)\
                        .then_inc(rstd_ready, 1)

            over_batches(pool, body)

        @block.vector
        def _(dve):
            dve.sem_inc(summed, 1)
            dve.sem_inc(y_used, 2)
            dve.sem_inc(agg_lo, 1)

            def transpose_rows(b, k, units=None):
                if units is not None:
                    dve.wait_ge(lo_ready, units)
                dve.wait_ge(rows_in[k % 2], (b * NT // 2 + k // 2 + 1) * 16 * QUADS)
                src = stage[:, k % 2, :, :].rearrange("p q (t c) -> p q t c", c=QP)
                dst = at[:, :, k * P:(k + 1) * P].rearrange("p t (q a) -> p q t a", a=QP)
                dve.transpose(dst, src).then_inc(transposed, 1)

            dve.wait_ge(w0_hi, 1)
            dve.tensor_tensor(w0s[:, :, 1, :], w0_in, w0s[:, :, 0, :].bitcast(F32), ALU.subtract)\
                .then_inc(w0_ready, 1)
            for k in range(NT):
                transpose_rows(0, k)

            def body(b, is_last):
                def split_feat(layer, t):
                    dve.wait_ge(feat_hi, b * 2 * NT + layer * NT + t + 1)
                    hi = feat[:, t, 0, :].bitcast(F32)
                    if layer == 0:
                        last = dve.scalar_tensor_tensor(feat[:, t, 1, :], x_in[:, t % XS, :], dinv[:, t:t + 1], hi,
                                                        op0=ALU.mult, op1=ALU.subtract)
                        last.then_inc(feat_lo, 1)
                    else:
                        dve.tensor_tensor(feat[:, t, 1, :], x1[:, t, :], hi, ALU.subtract).then_inc(feat_lo, 1)

                def split_agg(c):
                    dve.wait_ge(agg_hi, b * CPB + c + 1)
                    for ob in range(DK):
                        last = dve.tensor_tensor(agg[:, 1, ob, :], agg_ps[c % 2][ob][:, :],
                                                 agg[:, 0, ob, :].bitcast(F32), ALU.subtract)
                    last.then_inc(agg_lo, 1)

                def add_up(t):
                    dve.wait_ge(ylo_ready, b * NT + t + 1)
                    dve.scalar_tensor_tensor(x1[:, t, :], y_ps[t % TPC][:, 0:D], dinv[:, t:t + 1], y_lo[:, t % 2, :],
                                             op0=ALU.mult, op1=ALU.add).then_inc(y_used, 1)
                    dve.wait_ge(biased, b * NT + t + 1)
                    dve.wait_ge(y_used, b * NT + t + 3)
                    last = dve.tensor_tensor(x1[:, t, :], x1[:, t, :], x_in[:, t % XS, :], ALU.add)
                    last.then_inc(summed, 1)
                    dve.wait_ge(summed, b * NT + t + 2)
                    dve.bn_stats(stats[:, :], x1[:, t, :]).then_inc(stats_done, 1)
                    dve.wait_ge(stats_done, b * NT + t + 1)
                    dve.memset(wait_here[:, :], 0.0)
                    last = dve.bn_aggr(mean_var[:, t % TPC, :], stats[:, :])
                    if t % TPC == TPC - 1:
                        last.then_inc(var_ready, 1)

                def normalise(j):
                    dve.wait_ge(rstd_ready, b * NJ + j + 1)
                    for i in range(TPC):
                        t = TPC * j + i
                        dve.tensor_scalar(x1[:, t, :], x1[:, t, :], mean_var[:, i, 0:1], rstd[:, i:i + 1],
                                          op0=ALU.subtract, op1=ALU.mult).then_inc(x1_ready, 1)

                def add_eps(j):
                    for t in range(TPC * j, TPC * (j + 1)):
                        diag = at[:, t, t * P:(t + 1) * P]
                        dve.scalar_tensor_tensor(diag, ident[:, :], eps_sb[:, 0:1], diag, op0=ALU.mult,
                                                 op1=ALU.add).then_inc(eps_added, 1)

                dve.wait_ge(sums_folded, b + 1)
                folded = fold_ps[:, 0:NT * QUADS].rearrange("p (t q) -> p t q", q=QUADS)
                for q in range(QUADS):
                    rows = slice(q * QP, (q + 1) * QP)
                    last = dve.tensor_scalar(deg[rows, :], folded[rows, :, q], DEG_EPS, None, op0=ALU.add)
                last.then_inc(deg_ready, 1)

                for layer in range(2):
                    for j in range(NJ):
                        c = layer * NJ + j
                        for u in range(UPC):
                            if (layer == 0 and j or c == NJ) and u == 3:
                                add_eps(j - 1 if layer == 0 else NJ - 1)
                            if j == 0 and u == 2:
                                for t in range(2):
                                    split_feat(layer, t)
                            if c and u == 2:
                                split_agg(c - 1)
                            if j == 0:
                                for t in feats_before(u):
                                    if t >= 2:
                                        split_feat(layer, t)
                            if 2 <= c <= NJ and u == 1:
                                normalise(c - 2)
                            if layer == 0 and j and u >= 4:
                                add_up(TPC * (j - 1) + u - 4)
                            if c == NJ and u == 4:
                                for i in range(TPC):
                                    add_up(TPC * (NJ - 1) + i)
                            if c == NJ and u == 5:
                                normalise(NJ - 1)
                            if layer and not is_last:
                                for k in tiles_behind(j, u):
                                    transpose_rows(b + 1, k, b * UNITS + LU + UPC * j)
                            dve.wait_ge(hi_ready, b * UNITS + layer * LU + j * UPC + u + 1)
                            dve.tensor_tensor(ring_view(unit_lo, layer, j, u), at_unit(layer, j, u),
                                              ring_view(unit_hi, layer, j, u).bitcast(F32),
                                              ALU.subtract).then_inc(lo_ready, 1)
                if not is_last:
                    for k in range(NT - TPC, NT):
                        transpose_rows(b + 1, k, (b + 1) * UNITS)
                split_agg(CPB - 1)

            over_batches(dve, body)

        @block.tensor
        def _(pe):
            pe.sem_inc(unit_free, RING)
            pe.wait_ge(w0_ready, 1)
            pe.wait_ge(pool_consts, 3 + 2 * QUADS - 1)

            def body(b, is_last):
                pe.wait_ge(rows_summed, (b + 1) * NT)
                pe.wait_ge(y_used, b * NT + 2)
                pe.matmul(fold_ps[:, 0:NT * QUADS], fold[:, :], part[:, :, :].rearrange("p t q -> p (t q)"),
                          start=True, stop=True).then_inc(sums_folded, 1)

                def times_w(j):
                    pe.wait_ge(agg_lo, b * CPB + j + 2)
                    if j == 0:
                        pe.wait_ge(deg_ready, b + 1)
                    pe.wait_ge(y_used, b * NT + TPC * j + 2)
                    for i in range(TPC):
                        cols = slice(i * P, (i + 1) * P)
                        for k in range(DK):
                            pe.matmul(y_ps[i][:, :], agg[:, 0, k, cols], w0s[:, k, :, :].rearrange("p h d -> p (h d)"),
                                      start=(k == 0), stop=False)
                            last = pe.matmul(y_ps[i][:, 0:D], agg[:, 1, k, cols], w0s[:, k, 0, :],
                                             start=False, stop=(k == DK - 1))
                        last.then_inc(y_ready, 1)

                for layer in range(2):
                    for j in range(NJ):
                        c = layer * NJ + j
                        for u in range(UPC):
                            if u == 2 and 1 <= c <= NJ:
                                times_w(c - 1)
                            if u == 0:
                                pe.wait_ge(agg_lo, b * CPB + max(c - 2, -1) + 2)
                            pe.wait_ge(lo_ready, b * UNITS + layer * LU + j * UPC + u + 1)
                            if j == 0:
                                pe.wait_ge(feat_lo, b * 2 * NT + layer * NT + UT * (u + 1))
                            hi, lo = ring_view(unit_hi, layer, j, u), ring_view(unit_lo, layer, j, u)
                            for tt in range(UT):
                                t = UT * u + tt
                                for ob in range(DK):
                                    out = agg_ps[c % 2][ob][:, :]
                                    f_hi = feat[:, t, 0, ob * P:(ob + 1) * P]
                                    f_lo = feat[:, t, 1, ob * P:(ob + 1) * P]
                                    pe.matmul(out, f_hi, hi[:, tt, :], start=(t == 0), stop=False)
                                    pe.matmul(out, f_hi, lo[:, tt, :], start=False, stop=False)
                                    last = pe.matmul(out, f_lo, hi[:, tt, :], start=False, stop=(t == NT - 1))
                            last.then_inc(unit_free, 1)

            over_batches(pe, body)


def dense(nc, g):
    B, D, H, CH, NJ, TPC, DK, HK = (g[k] for k in ("B", "D", "H", "CH", "NJ", "TPC", "DK", "HK"))
    agg_scratch, x1_scratch, y_rows = g["agg_scratch"], g["x1_scratch"], g["y_rows"]
    ident, psum = g["ident"], g["psum"]
    NC = B * NJ

    with ExitStack() as ctx:
        def sb(name, shape, dt=F32):
            return ctx.enter_context(nc.sbuf_tensor(name, shape, dt))

        def sem(name):
            return ctx.enter_context(nc.semaphore(name))

        w1_in = sb("w1_in", [P, DK, H])
        w2_in = sb("w2_in", [P, HK, D])
        w1s = sb("w1s", [P, 2, DK, H], F32R)
        w2s = sb("w2s", [P, HK, 2, D], F32R)
        b1_sb = sb("b1_sb", [P, HK])
        rms_sb = sb("rms_sb", [P, HK])
        b2_sb = sb("b2_sb", [P, D])
        ones = sb("ones", [P, P])
        minus_half4 = sb("minus_half4", [P, TPC])
        wait_here2 = sb("wait_here2", [P, 1])
        ln_eps4 = sb("ln_eps4", [P, TPC])
        agg_in = sb("agg_in", [P, 2, 2, DK, CH], F32R)
        x1_in = sb("x1_in", [P, 2, TPC, D])
        hid = sb("hid", [P, 2, HK, CH])
        s_hi = sb("s_hi", [P, HK, CH], F32R)
        s_lo = sb("s_lo", [P, HK, CH], F32R)
        sq = sb("sq", [P, HK, CH])
        sum_sq = sb("sum_sq", [P, 2, CH])
        mean_sq = sb("mean_sq", [P, TPC])
        rms_inv = sb("rms_inv", [P, TPC])
        diag = sb("diag", [P, CH])
        out = sb("out", [P, 2, TPC, D])
        bstats = sb("bstats", [P, TPC, 6])
        mv = sb("mv", [P, TPC, 2])
        vare = sb("vare", [P, TPC])
        rstd2 = sb("rstd2", [P, TPC])

        h_ps = psum[0:2]
        o_ps = psum[2:6]
        sq_ps = psum[6]
        r_ps = psum[7]

        weights_in = sem("weights_in")
        w_hi = sem("w_hi")
        w_ready = sem("w_ready")
        ones_set = sem("ones_set")
        agg_here = [sem(f"agg_here{s}") for s in range(2)]
        x1_here = [sem(f"x1_here{s}") for s in range(2)]
        h_done = sem("h_done")
        h_ready = sem("h_ready")
        squared = sem("squared")
        sq_added = sem("sq_added")
        sq_summed = sem("sq_summed")
        mean_ready = sem("mean_ready")
        rms_ready = sem("rms_ready")
        diag_ready = sem("diag_ready")
        r_spread = sem("r_spread")
        z_ready = sem("z_ready")
        act_ready = sem("act_ready")
        shi_ready = sem("shi_ready")
        slo_ready = sem("slo_ready")
        w2_done = sem("w2_done")
        x1_biased = sem("x1_biased")
        half_added = sem("half_added")
        o_read = sem("o_read")
        o_stats = sem("o_stats")
        o_var = sem("o_var")
        vare_ready = sem("vare_ready")
        rstd2_ready = sem("rstd2_ready")
        out_ready = sem("out_ready")
        out_stored = [sem(f"out_stored{s}") for s in range(2)]
        block = ctx.enter_context(nc.Block())

        def wait(eng, semaphore, value):
            if not isinstance(value, int) or value > 0:
                eng.wait_ge(semaphore, value)

        def over_steps(eng, step):
            for o in range(NJ):
                step(0, o)
            if B > 2:
                with eng.Fori(1, B) as m:
                    for o in range(NJ):
                        step(m, o)
            elif B == 2:
                for o in range(NJ):
                    step(1, o)
            for o in range(3):
                step(B, o)

        def there(m, o, back):
            if isinstance(m, int):
                return 0 <= NJ * m + o - back < NC
            return True

        def used(m, o):
            return m * (NJ // 2) + o // 2

        @block.sync
        def _(sp):
            sp.dma_start(w1_in[:, :, :], g["w1"].rearrange("(k p) h -> p k h", p=P)).then_inc(weights_in, 16)

            def load_agg(m, o):
                wait(sp, h_done, (NJ * m + o - 1) * HK)
                sp.dma_start(agg_in[:, o % 2, :, :, :].bitcast(F32).rearrange("p h k n -> p (h k n)"),
                             agg_scratch[NJ * m + o]).then_inc(agg_here[o % 2], 16)

            load_agg(0, 0)
            sp.dma_start(w2_in[:, :, :], g["w2"].rearrange("(h p) d -> p h d", p=P)).then_inc(weights_in, 16)
            sp.dma_start(b2_sb[:, :], g["b2"].to_broadcast([P, D])).then_inc(weights_in, 16)
            with nc.allow_non_contiguous_dma(reason="a hidden unit's bias and weight go to its partition"):
                sp.dma_start(b1_sb[:, :], g["b1"].rearrange("(h p) -> p h", p=P)).then_inc(weights_in, 16)
                sp.dma_start(rms_sb[:, :], g["rms_w"].rearrange("(h p) -> p h", p=P)).then_inc(weights_in, 16)

            def step(m, o):
                if there(m, o, 0) and not (isinstance(m, int) and m == 0 and o == 0):
                    load_agg(m, o)
                if there(m, o, 2):
                    wait(sp, half_added, (NJ * m + o - 3) * TPC)
                    sp.dma_start(x1_in[:, o % 2, :, :].rearrange("p t d -> p (t d)"),
                                 x1_scratch[NJ * m + o - 2]).then_inc(x1_here[o % 2], 16)
                if there(m, o, 3):
                    b, j = (m, o - 3) if o >= 3 else (m - 1, o - 3 + NJ)
                    for t in range(TPC):
                        wait(sp, out_ready, (NJ * m + o - 3) * TPC + t + 1)
                        sp.dma_start(y_rows[b, TPC * j + t], out[:, (o - 3) % 2, t, :])\
                            .then_inc(out_stored[(o - 3) % 2], 16)

            over_steps(sp, step)
            for s in range(2):
                sp.wait_ge(out_stored[s], NC // 2 * TPC * 16)

        @block.scalar
        def _(act):
            act.wait_ge(weights_in, 5 * 16)
            act.copy(w1s[:, 0, :, :], w1_in[:, :, :]).then_inc(w_hi, 1)
            act.copy(w2s[:, :, 0, :], w2_in[:, :, :]).then_inc(w_hi, 1)

            def activate(m, o, h):
                n = (NJ * m + o) * HK + h
                cur = hid[:, o % 2, h, :]
                act.wait_ge(z_ready, n + 1)
                act.activation(cur, cur, ACT.Silu, scale=rms_sb[:, h:h + 1]).then_inc(act_ready, 1)
                act.wait_ge(act_ready, n + 1)
                wait(act, w2_done, n - HK + 1)
                act.copy(s_hi[:, h, :], cur).then_inc(shi_ready, 1)

            def square(m, o, h):
                i = NJ * m + o
                act.wait_ge(h_ready, i * HK + h + 1)
                if h == 0:
                    wait(act, sq_summed, i - 1)
                else:
                    wait(act, sq_added, (i - 1) * (HK - 1) + h)
                dst = sq[:, h, :] if h else sum_sq[:, o % 2, :]
                act.activation(dst, hid[:, o % 2, h, :], ACT.Square).then_inc(squared, 1)

            def step(m, o):
                i = NJ * m + o
                if there(m, o, 0):
                    for h in range(HK):
                        act.wait_ge(h_done, i * HK + h + 1)
                        wait(act, slo_ready, (i - 2) * HK + h + 1)
                        act.activation(hid[:, o % 2, h, :], h_ps[h % 2][:, :], ACT.Identity,
                                       bias=b1_sb[:, h:h + 1]).then_inc(h_ready, 1)
                        if h:
                            square(m, o, h - 1)
                    square(m, o, HK - 1)
                if there(m, o, 1):
                    for h in range(HK):
                        activate(m, o - 1, h)

            over_steps(act, step)

        @block.gpsimd
        def _(pool):
            pool.memset(ones[:, :], 1.0).then_inc(ones_set, 1)
            pool.memset(minus_half4[:, :], -0.5).then_inc(ones_set, 1)
            pool.memset(ln_eps4[:, :], LN_EPS).then_inc(ones_set, 1)
            pool.wait_ge(ones_set, 3)
            pool.wait_ge(weights_in, 5 * 16)

            def add_square(m, o, h):
                i = NJ * m + o
                pool.wait_ge(squared, i * HK + h + 1)
                wait(pool, sq_added, i * (HK - 1) + h - 1)
                pool.tensor_tensor(sum_sq[:, o % 2, :], sum_sq[:, o % 2, :], sq[:, h, :], ALU.add)\
                    .then_inc(sq_added, 1)

            def step(m, o):
                i = NJ * m + o
                if there(m, o, 1):
                    pool.wait_ge(mean_ready, i)
                    pool.tensor_tensor(rms_inv[:, :], mean_sq[:, :], minus_half4[:, :], ALU.pow).then_inc(rms_ready, 1)
                if there(m, o, 0):
                    for h in (1, 2):
                        add_square(m, o, h)
                if there(m, o, 3):
                    pool.wait_ge(o_var, i - 2)
                    pool.tensor_tensor(vare[:, :], mv[:, :, 1], ln_eps4[:, :], ALU.add).then_inc(vare_ready, 1)
                    pool.wait_ge(vare_ready, i - 2)
                    pool.tensor_tensor(rstd2[:, :], vare[:, :], minus_half4[:, :], ALU.pow).then_inc(rstd2_ready, 1)
                if there(m, o, 0):
                    for h in range(3, HK):
                        add_square(m, o, h)
                if there(m, o, 2):
                    p = o % 2
                    pool.wait_ge(x1_here[p], (used(m, o - 2) + 1) * 16)
                    for t in range(TPC):
                        pool.tensor_tensor(x1_in[:, p, t, :], x1_in[:, p, t, :], b2_sb[:, :], ALU.add)\
                            .then_inc(x1_biased, 1)

            over_steps(pool, step)

        @block.vector
        def _(dve):
            dve.wait_ge(w_hi, 1)
            dve.tensor_tensor(w1s[:, 1, :, :], w1_in[:, :, :], w1s[:, 0, :, :].bitcast(F32), ALU.subtract)\
                .then_inc(w_ready, 1)
            dve.wait_ge(w_hi, 2)
            dve.tensor_tensor(w2s[:, :, 1, :], w2_in[:, :, :], w2s[:, :, 0, :].bitcast(F32), ALU.subtract)\
                .then_inc(w_ready, 1)

            def scale(m, o, h):
                cur = hid[:, o % 2, h, :]
                if h == 0:
                    dve.wait_ge(r_spread, NJ * m + o + 1)
                dve.tensor_tensor(cur, cur, r_ps[:, :], ALU.mult).then_inc(z_ready, 1)

            def split(m, o, h):
                dve.wait_ge(shi_ready, (NJ * m + o) * HK + h + 1)
                dve.tensor_tensor(s_lo[:, h, :], hid[:, o % 2, h, :], s_hi[:, h, :].bitcast(F32), ALU.subtract)\
                    .then_inc(slo_ready, 1)

            def add_up(m, o, t):
                n = (NJ * m + o) * TPC + t
                v = out[:, o % 2, t, :]
                if t == 0:
                    dve.wait_ge(w2_done, (NJ * m + o + 1) * HK)
                    wait(dve, out_stored[o % 2], used(m, o) * TPC * 16)
                dve.wait_ge(x1_biased, n + 1)
                dve.tensor_tensor(v, o_ps[t][:, 0:D], x1_in[:, o % 2, t, :], ALU.add).then_inc(half_added, 1)
                dve.wait_ge(half_added, n + 1)
                dve.tensor_tensor(v, v, o_ps[t][:, D:2 * D], ALU.add).then_inc(o_read, 1)
                dve.wait_ge(o_read, n + 1)
                dve.bn_stats(bstats[:, t, :], v).then_inc(o_stats, 1)
                dve.wait_ge(o_stats, n + 1)
                dve.memset(wait_here2[:, :], 0.0)
                last = dve.bn_aggr(mv[:, t, :], bstats[:, t, :])
                if t == TPC - 1:
                    last.then_inc(o_var, 1)

            def step(m, o):
                i = NJ * m + o
                if there(m, o, 3):
                    add_up(m, o - 3, 0)
                if there(m, o, 1):
                    dve.wait_ge(sq_summed, i)
                    dve.tensor_scalar(mean_sq[:, :], sq_ps[:, 0:TPC], 1.0 / H, RMS_EPS, op0=ALU.mult,
                                      op1=ALU.add).then_inc(mean_ready, 1)
                if there(m, o, 3):
                    add_up(m, o - 3, 1)
                if there(m, o, 1):
                    dve.wait_ge(rms_ready, i)
                    wait(dve, r_spread, i - 1)
                    for t in range(TPC):
                        last = dve.tensor_scalar(diag[:, t * P:(t + 1) * P], ident[:, :], rms_inv[:, t:t + 1], None,
                                                 op0=ALU.mult)
                    last.then_inc(diag_ready, 1)
                if there(m, o, 3):
                    add_up(m, o - 3, 2)
                    add_up(m, o - 3, 3)
                if there(m, o, 1):
                    for h in range(2):
                        scale(m, o - 1, h)
                if there(m, o, 3):
                    dve.wait_ge(rstd2_ready, i - 2)
                    for t in range(TPC):
                        v = out[:, (o - 3) % 2, t, :]
                        dve.tensor_scalar(v, v, mv[:, t, 0:1], rstd2[:, t:t + 1], op0=ALU.subtract,
                                          op1=ALU.mult).then_inc(out_ready, 1)
                if there(m, o, 1):
                    for h in range(2, HK):
                        scale(m, o - 1, h)
                        split(m, o - 1, h - 2)
                    for h in (HK - 2, HK - 1):
                        split(m, o - 1, h)

            over_steps(dve, step)

        @block.tensor
        def _(pe):
            pe.wait_ge(ones_set, 3)

            def sum_squares(m, o):
                i = NJ * m + o
                pe.wait_ge(sq_added, (i + 1) * (HK - 1))
                wait(pe, mean_ready, i)
                for t in range(TPC):
                    last = pe.matmul(sq_ps[:, t:t + 1], sum_sq[:, o % 2, t * P:(t + 1) * P], ones[:, 0:1],
                                     start=True, stop=True)
                last.then_inc(sq_summed, 1)

            def spread_rms(m, o):
                i = NJ * m + o
                pe.wait_ge(diag_ready, i + 1)
                wait(pe, z_ready, i * HK)
                pe.matmul(r_ps[:, :], ones[:, :], diag[:, :], start=True, stop=True).then_inc(r_spread, 1)

            def step(m, o):
                i = NJ * m + o
                if there(m, o, 0):
                    pe.wait_ge(agg_here[o % 2], (used(m, o) + 1) * 16)
                    if isinstance(m, int) and m == 0 and o == 0:
                        pe.wait_ge(w_ready, 1)
                    a_hi = agg_in[:, o % 2, 0, :, :]
                    a_lo = agg_in[:, o % 2, 1, :, :]
                for h in range(HK):
                    if there(m, o, 0):
                        wait(pe, h_ready, i * HK + h - 1)
                        bank = h_ps[h % 2][:, :]
                        cols = slice(h * P, (h + 1) * P)
                        for k in range(DK):
                            pe.matmul(bank, w1s[:, 0, k, cols], a_hi[:, k, :], start=(k == 0), stop=False)
                            pe.matmul(bank, w1s[:, 0, k, cols], a_lo[:, k, :], start=False, stop=False)
                            last = pe.matmul(bank, w1s[:, 1, k, cols], a_hi[:, k, :], start=False, stop=(k == DK - 1))
                        last.then_inc(h_done, 1)
                    if there(m, o, 1) and h == 1:
                        sum_squares(m, o - 1)
                    if there(m, o, 1) and h == 5:
                        spread_rms(m, o - 1)
                if there(m, o, 2):
                    wait(pe, o_read, (i - 2) * TPC)
                    if isinstance(m, int) and i == 2:
                        pe.wait_ge(w_ready, 2)
                    for h in range(HK):
                        pe.wait_ge(slo_ready, (i - 2) * HK + h + 1)
                        for t in range(TPC):
                            cols = slice(t * P, (t + 1) * P)
                            pe.matmul(o_ps[t][:, :], s_hi[:, h, cols], w2s[:, h, :, :].rearrange("p s d -> p (s d)"),
                                      start=(h == 0), stop=False)
                            last = pe.matmul(o_ps[t][:, 0:D], s_lo[:, h, cols], w2s[:, h, 0, :],
                                             start=False, stop=(h == HK - 1))
                        last.then_inc(w2_done, 1)

            over_steps(pe, step)


_OUT = ((8, 2048, 256), "float32")


def kernel(x, adj, L0_gnn_weight, L0_gnn_bias, L1_gnn_epsilon, L1_gnn_W1, L1_gnn_b1, L1_gnn_rms_weight, L1_gnn_W2,
           L1_gnn_b2):
    import numpy as np
    import concourse.bacc as bacc
    from concourse.bass_utils import run_bass_kernel_spmd

    nc = bacc.Bacc("TRN2", target_bir_lowering=False, num_devices=1, dynamic_dma_scratch_size=1024)
    arrays = {
        "x": np.asarray(x),
        "adj": np.asarray(adj),
        "w0": np.asarray(L0_gnn_weight),
        "bias0": np.asarray(L0_gnn_bias).reshape(1, -1),
        "eps": np.asarray(L1_gnn_epsilon).reshape(1, 1),
        "w1": np.asarray(L1_gnn_W1),
        "b1": np.asarray(L1_gnn_b1),
        "rms_w": np.asarray(L1_gnn_rms_weight),
        "w2": np.asarray(L1_gnn_W2),
        "b2": np.asarray(L1_gnn_b2).reshape(1, -1),
    }
    args = {n: nc.dram_tensor(n, a.shape, mybir.dt.from_np(a.dtype), kind="ExternalInput").ap()
            for n, a in arrays.items()}
    y = nc.dram_tensor("y", _OUT[0], F32, kind="ExternalOutput").ap()
    build(nc, **args, y=y)
    results = run_bass_kernel_spmd(nc, [arrays], core_ids=[0]).results
    return results[0]["y"]
```

```python
from contextlib import ExitStack

import concourse.bass as bass
from concourse import mybir

F32 = mybir.dt.float32
F32R = mybir.dt.float32r
ALU = mybir.AluOpType
ACT = mybir.ActivationFunctionType
P = 128
QUADS = 4
QP = P // QUADS
LN_EPS = 1e-5
DEG_EPS = 1e-5
RMS_EPS = 1e-6


def build(nc, x, adj, w0, bias0, eps, w1, b1, rms_w, w2, b2, y):
    B, N, D = x.shape
    H = w1.shape[1]
    NT = N // P
    CH = 512
    NJ = N // CH
    TPC = CH // P
    DK = D // P
    HK = H // P
    QW = N // QUADS
    UT = 2
    UPC = NT // UT
    UNITS = 2 * NJ * UPC
    RING = 3
    assert D == 256 and QW == CH and UPC == 8 and TPC == QUADS and DK == 2

    adj_rows = adj.rearrange("b (Q k a) (q f) -> b k Q q a f", Q=QUADS, a=QP, q=QUADS)
    x_rows = x.rearrange("b (q t c) d -> b t q c d", q=QUADS, c=QP)
    y_rows = y.rearrange("b (q t c) d -> b t q c d", q=QUADS, c=QP)
    agg_scratch = nc.dram_tensor("agg_scratch", [B * NJ, P, 2 * DK * CH], F32)
    x1_scratch = nc.dram_tensor("x1_scratch", [B * NJ, P, TPC * D], F32)

    with ExitStack() as both:
        def keep(name, shape, dt=F32):
            return both.enter_context(nc.sbuf_tensor(name, shape, dt))

        def keep_sem(name):
            return both.enter_context(nc.semaphore(name))

        ident = keep("ident", [P, P])
        at_offset = nc.sbuf_base
        at = keep("at", [P, NT, N])

        def in_at(name, shape, block, dt=F32):
            return nc.alloc_sbuf_tensor_at(name, shape, dt, offset=at_offset + block * N * 4)

        w1s = in_at("w1s", [P, 2, DK, H], 0, F32R)
        w2s = in_at("w2s", [P, HK, 2, D], 2, F32R)
        agg_in = in_at("agg_in", [P, 2, 2, DK, CH], 4, F32R)
        stage = keep("stage", [P, 2, QUADS, CH])
        agg_offset = nc.sbuf_base
        agg = keep("agg", [P, 2, DK, CH], F32R)
        agg_rows = nc.alloc_sbuf_tensor_at("agg_rows", [P, QUADS, CH], F32, offset=agg_offset)
        b1_sb = keep("b1_sb", [P, HK])
        rms_sb = keep("rms_sb", [P, HK])
        agg_stored = keep_sem("agg_stored")
        agg_here = [keep_sem(f"agg_here{s}") for s in range(2)]
        w_ready = keep_sem("w_ready")
        psum = [both.enter_context(nc.psum_tensor(f"bank{i}", [P, CH], F32)) for i in range(8)]

        shared = locals()
        aggregate(nc, shared)
        dense(nc, shared)


SHIFTS = (12, 20)
LOAD_X = 12
TAIL = [(14, 'T'), (15, 'T'), (-1, 'deg'), (0, 'U'), (0, 'P'), (1, 'U'), (1, 'P'), (2, 'P')]
LATE_T = [12, 13]
POOL_UNITS = (0, 1, 7)
DVE_SUMS = (13,)
SUM_AT = {(0, 7): [0], (1, 1): [1], (1, 2): [2, 3], (1, 5): [4], (2, 0): [5, 6], (2, 2): [7], (2, 3): [8], (2, 5):
          [9], (3, 2): [10], (3, 4): [11, 12], (3, 6): [13], (4, 0): [14, 15]}
T_AT = {(1, 0): [0], (1, 1): [1, 2], (1, 4): [3], (2, 0): [4], (2, 1): [5, 6], (2, 5): [7], (3, 0): [8, 9], (3, 2):
        [10, 11]}
FEAT_PAIRS = {1: [4], 3: [5], 7: [6, 7]}
FOLD_U = 8


def aggregate(nc, g):
    B, N, D, NT, CH, NJ, TPC, DK, UT, UPC, UNITS, RING = (
        g[k] for k in ("B", "N", "D", "NT", "CH", "NJ", "TPC", "DK", "UT", "UPC", "UNITS", "RING"))
    adj_rows, x_rows, agg_scratch, x1_scratch = (
        g[k] for k in ("adj_rows", "x_rows", "agg_scratch", "x1_scratch"))
    ident, psum, at, w1s, w2s, stage, agg_in, agg, agg_rows = (
        g[k] for k in ("ident", "psum", "at", "w1s", "w2s", "stage", "agg_in", "agg", "agg_rows"))
    b1_sb, rms_sb, agg_stored, agg_here, w_ready = (
        g[k] for k in ("b1_sb", "rms_sb", "agg_stored", "agg_here", "w_ready"))
    last_batch = B - 1
    CPB = 2 * NJ
    LU = NJ * UPC
    XS = 4
    assert (UNITS + len(SHIFTS)) % RING == 0
    AHEAD = RING

    with ExitStack() as ctx:
        def sb(name, shape, dt=F32):
            return ctx.enter_context(nc.sbuf_tensor(name, shape, dt))

        def sem(name):
            return ctx.enter_context(nc.semaphore(name))

        feat_offset = nc.sbuf_base
        feat = sb("feat", [P, NT, 2, D], F32R)
        x1 = stage[:, :, :, :].rearrange("p s q f -> p (s q f)").rearrange("p (t d) -> p t d", d=D)
        unit_hi = sb("unit_hi", [P, RING, UT * CH], F32R)
        unit_lo = sb("unit_lo", [P, RING, UT * CH], F32R)
        w0s = sb("w0s", [P, DK, 2, D], F32R)
        fold = sb("fold", [P, P])
        bias = sb("bias", [P, D])
        eps_sb = sb("eps_sb", [P, 1])
        third = sb("third", [P, QUADS, CH])
        x_in = third[:, 0:2, :].rearrange("p q (s d) -> p (q s) d", d=D)
        y_lo = third[:, 2, :].rearrange("p (s d) -> p s d", d=D)
        part = sb("part", [P, NT, QUADS])
        deg = sb("deg", [P, NT])
        dinv = sb("dinv", [P, NT])
        minus_half = sb("minus_half", [P, NT])
        wait_here = sb("wait_here", [P, 1])
        ln_eps = sb("ln_eps", [P, TPC])
        stats = sb("stats", [P, 6])
        mean_var = sb("mean_var", [P, TPC, 2])
        var_eps = sb("var_eps", [P, TPC])
        rstd = sb("rstd", [P, TPC])
        w0_in = x_in[:, 0:DK, :]
        w1_in = stage[:, 0, :, :].rearrange("p (k i) n -> p k (i n)", k=DK)
        w2_in = stage[:, 1, :, :].rearrange("p q (i d) -> p (q i) d", d=D)

        agg_ps = [[psum[2 * s + ob] for ob in range(DK)] for s in range(2)]
        y_ps = psum[4:8]
        fold_ps = psum[7]

        places = [stage[:, 0, :, :], stage[:, 1, :, :],
                  nc.alloc_sbuf_tensor_at("feat_rows", [P, QUADS, CH], F32, offset=feat_offset)[:, :, :],
                  agg_rows[:, :, :], third[:, :, :]]
        FEAT_PLACE, AGG_PLACE, THIRD_PLACE = 2, 3, 4
        FIRST_PLACES = [0, 1, FEAT_PLACE, AGG_PLACE] * (NT // 4)
        LATER_PLACES = [0, THIRD_PLACE, 1] * 3 + [0, THIRD_PLACE, 1, 0, 1, FEAT_PLACE, AGG_PLACE]

        rows_in = [sem(f"rows_in{s}") for s in range(len(places))]
        x_loaded = [sem(f"x_loaded{s}") for s in range(XS)]
        consts_in = sem("consts_in")
        pool_consts = sem("pool_consts")
        w0_hi = sem("w0_hi")
        w0_ready = sem("w0_ready")
        act_summed = sem("act_summed")
        dve_summed = sem("dve_summed")
        transposed = sem("transposed")
        sums_folded = sem("sums_folded")
        deg_ready = sem("deg_ready")
        dinv_ready = sem("dinv_ready")
        hi_ready = sem("hi_ready")
        dve_lo = sem("dve_lo")
        pool_lo = sem("pool_lo")
        unit_free = sem("unit_free")
        feat_hi = sem("feat_hi")
        feat_lo = sem("feat_lo")
        agg_hi = sem("agg_hi")
        agg_lo = sem("agg_lo")
        w_in = sem("w_in")
        w_hi = sem("w_hi")
        y_ready = sem("y_ready")
        ylo_ready = sem("ylo_ready")
        y_used = sem("y_used")
        biased = sem("biased")
        summed = sem("summed")
        stats_done = sem("stats_done")
        var_ready = sem("var_ready")
        veps_ready = sem("veps_ready")
        rstd_ready = sem("rstd_ready")
        x1_ready = sem("x1_ready")
        x1_stored = [sem(f"x1_stored{h}") for h in range(2)]
        eps_added = sem("eps_added")
        block = ctx.enter_context(nc.Block())

        def over_batches(eng, body):
            with eng.Fori(0, last_batch) as b:
                body(b, False)
            body(last_batch, True)


        def slot_of(v):
            return (v + (v >= SHIFTS[0]) + (v >= SHIFTS[1])) % RING

        def units_before(v):
            return max(w for w in range(v - UNITS, v) if slot_of(w % UNITS) == slot_of(v)) + 1

        def at_unit(layer, j, u):
            return at[:, UT * u:UT * u + UT, j * CH:(j + 1) * CH]

        def ring_view(ring, layer, j, u):
            return ring[:, slot_of(layer * LU + j * UPC + u), :].rearrange("p (t n) -> p t n", t=UT)

        def pool_splits(layer, j, u):
            return layer == 1 and j >= 1 and u in POOL_UNITS

        def pool_units(n):
            return sum(pool_splits(v // LU, v % LU // UPC, v % UPC) for v in range(n))

        POOL_TOTAL = pool_units(UNITS)

        def wait_lo(eng, b, n):
            p = pool_units(n)
            if n - p:
                eng.wait_ge(dve_lo, b * (UNITS - POOL_TOTAL) + n - p)
            if p:
                eng.wait_ge(pool_lo, b * POOL_TOTAL + p)


        def place_of(k, first):
            return FIRST_PLACES[k] if first else LATER_PLACES[k]

        def before_in_place(k, first):
            return max((n for n in range(k) if place_of(n, first) == place_of(k, first)), default=None)

        def rows_here(b, k, first):
            s = place_of(k, first)
            loads = (FIRST_PLACES if first else LATER_PLACES)[:k + 1].count(s)
            if not first:
                loads += FIRST_PLACES.count(s) + b * LATER_PLACES.count(s)
            return rows_in[s], loads * 16 * QUADS

        def last_rows_here(b, k):
            s = place_of(k, False)
            assert s == place_of(k, True) and k == max(n for n in range(NT) if LATER_PLACES[n] == s)
            return rows_in[s], (FIRST_PLACES.count(s) + b * LATER_PLACES.count(s)) * 16 * QUADS

        def rows_view(k, first):
            return places[place_of(k, first)]

        ACT_TILES = NT - len(DVE_SUMS)

        def sums(b, k):
            d = sum(n <= k for n in DVE_SUMS)
            if k in DVE_SUMS:
                return dve_summed, b * len(DVE_SUMS) + d
            return act_summed, b * ACT_TILES + k + 1 - d

        T_ORDER = list(range(NT - TPC)) + [k for k, _ in TAIL if k >= 0 and _ == "T"] + LATE_T

        def steps():
            for layer in range(2):
                for j in range(NJ):
                    for u in range(UPC):
                        if layer or j or u >= AHEAD:
                            yield layer, j, u

        def feats_at(layer, j, u):
            if layer == 0 and j == 0:
                return [(0, t) for t in range(UT * u, UT * u + UT)]
            if layer == 0 and j == NJ - 1 and u >= RING + 1:
                p = u - RING - 1
                return [(1, t) for t in range(UT * p, UT * p + UT)]
            if layer == 1 and j == 0:
                pairs = FEAT_PAIRS.get(u, [])
                return [(1, t) for p in pairs for t in range(UT * p, UT * p + UT)]
            return []

        def scaled_at(layer, j, u):
            c = layer * NJ + j
            if c == NJ:
                now = {4: [0, 1], 5: [2, 3]}.get(u, [])
                late = [TPC * (c - 2) + 3] if u == 0 else []
                return late + [TPC * (c - 1) + i for i in now]
            if layer:
                return []
            out = []
            if c >= 2 and u == 0:
                out.append(TPC * (c - 2) + 3)
            if c >= 1 and u >= 5:
                out.append(TPC * (c - 1) + u - 5)
            return out

        def normalised_at(layer, j, u):
            c = layer * NJ + j
            if 2 <= c <= NJ and u == 1:
                return [c - 2]
            if c == NJ and u == 6:
                return [NJ - 1]
            return []

        def summed_at(j, u):
            return SUM_AT.get((j, u), [])

        def transposed_at(j, u):
            return T_AT.get((j, u), [])

        @block.sync
        def _(sp):
            sp.dma_start(w0_in, g["w0"].rearrange("(k p) d -> p k d", p=P)).then_inc(consts_in, 16)
            sp.dma_start(bias[:, :], g["bias0"].to_broadcast([P, D])).then_inc(consts_in, 16)
            sp.dma_start(eps_sb[:, :], g["eps"].to_broadcast([P, 1])).then_inc(consts_in, 16)
            with nc.allow_non_contiguous_dma(reason="a hidden unit's bias and weight go to its partition"):
                sp.dma_start(b1_sb[:, :], g["b1"].rearrange("(h p) -> p h", p=P)).then_inc(consts_in, 16)
                sp.dma_start(rms_sb[:, :], g["rms_w"].rearrange("(h p) -> p h", p=P)).then_inc(consts_in, 16)

            def wait_all(*waits):
                values = [v if isinstance(v, int) else sp.to_reg(v) for _, v in waits]
                for (semaphore, _), value in zip(waits, values):
                    sp.wait_ge(semaphore, value)

            def load_rows(b, k, first, *waits):
                rows = [adj_rows[b, k, q] for q in range(QUADS)]
                wait_all(*waits)
                for q in range(QUADS):
                    sp.dma_start(rows_view(k, first)[:, q, :], rows[q]).then_inc(rows_in[place_of(k, first)], 16)

            def rows_used(b, k):
                return sums(b, k), (transposed, b * NT + T_ORDER.index(k) + 1)

            def load_x(b, t, residual, *waits):
                if residual and t < XS:
                    free = feat_lo, b * 2 * NT + NT - XS + t + 1
                elif residual:
                    free = summed, b * NT + t - XS + 2
                elif t < XS:
                    free = summed, b * NT + 1
                else:
                    free = feat_lo, b * 2 * NT + t - XS + 1
                src = x_rows[b, t]
                wait_all(*waits, free)
                sp.dma_start(x_in[:, t % XS, :], src).then_inc(x_loaded[t % XS], 16)

            def store_x1(b, j):
                dst = x1_scratch[b * NJ + j]
                src = x1[:, TPC * j:TPC * (j + 1), :].rearrange("p t d -> p (t d)")
                sp.wait_ge(x1_ready, b * NT + TPC * (j + 1))
                sp.dma_start(dst, src).then_inc(x1_stored[j // 2], 16)

            def half_stored(b, h):
                return (x1_stored[h], (b + 1) * (NJ // 2) * 16), (feat_lo, b * 2 * NT + NT + (h + 1) * (NT // 2))

            for k in range(NT):
                before = before_in_place(k, True)
                load_rows(0, k, True, *([] if before is None else rows_used(0, before)))
                if k == TPC:
                    for t in range(XS):
                        load_x(0, t, False, (w0_ready, 1))

            def body(b, is_last):
                if not is_last:
                    sp.to_reg(b * (N * D) * 4)
                for t in range(XS, NT):
                    load_x(b, t, False)
                for j in range(NJ):
                    for t in range(TPC * j, TPC * (j + 1)):
                        load_x(b, t, True)
                    if j:
                        store_x1(b, j - 1)
                if is_last:
                    store_x1(b, NJ - 1)
                    load_for_dense()
                    return
                load_rows(b + 1, 0, False, *half_stored(b, 0))
                store_x1(b, NJ - 1)
                load_rows(b + 1, 1, False, (summed, (b + 1) * NT + 1))
                load_rows(b + 1, 2, False, *half_stored(b, 1))
                for k in range(3, NT - 2):
                    load_rows(b + 1, k, False, *rows_used(b + 1, before_in_place(k, False)))
                    if k == LOAD_X:
                        last_third = max(n for n in range(NT) if LATER_PLACES[n] == THIRD_PLACE)
                        for t in range(XS):
                            load_x(b + 1, t, False, *rows_used(b + 1, last_third))
                load_rows(b + 1, NT - 2, False, (unit_free, (b + 1) * UNITS - UPC + 4 // UT + RING))
                load_rows(b + 1, NT - 1, False, (agg_stored, (b * NJ + NJ) * 16))

            def load_for_dense():
                sp.wait_ge(x1_stored[0], B * (NJ // 2) * 16)
                sp.wait_ge(x1_stored[1], B * (NJ // 2) * 16)
                sp.wait_ge(feat_lo, B * 2 * NT)
                sp.dma_start(w1_in, g["w1"].rearrange("(k p) h -> p k h", p=P)).then_inc(w_in, 16)
                sp.dma_start(w2_in, g["w2"].rearrange("(h p) d -> p h d", p=P)).then_inc(w_in, 16)
                wait_lo(sp, last_batch, LU + (NJ - 1) * UPC + 3)
                sp.wait_ge(agg_stored, 3 * 16)
                for i in range(2):
                    sp.dma_start(agg_in[:, i, :, :, :].bitcast(F32).rearrange("p h k n -> p (h k n)"), agg_scratch[i])\
                        .then_inc(agg_here[i], 16)

            over_batches(sp, body)
            for stored in x1_stored:
                sp.wait_ge(stored, B * NJ // 2 * 16)

        @block.scalar
        def _(act):
            def sum_rows(b, k, first):
                if k in DVE_SUMS:
                    return
                act.wait_ge(*rows_here(b, k, first))
                _, count = sums(b if first else b + 1, k)
                if not (first and k == 0):
                    act.wait_ge(act_summed, count - 1)
                if k == 0 and not first:
                    act.wait_ge(y_used, (b + 1) * NT + 2)
                for q in range(QUADS):
                    last = act.activation(y_ps[q][:, :], rows_view(k, first)[:, q, :], ACT.Copy,
                                          accum_out=part[:, k, q:q + 1])
                last.then_inc(act_summed, 1)

            def split_feat(b, layer, t):
                if layer == 1 or t < AHEAD * UT and not (isinstance(b, int) and b == 0):
                    act.wait_ge(unit_free, b * UNITS + layer * LU - UPC + t // UT + 1 + RING)
                if layer == 0:
                    if t in (0, TPC):
                        act.wait_ge(dinv_ready, 2 * b + (1 if t == 0 else 2))
                    if t == 0:
                        act.wait_ge(transposed, b * NT + T_ORDER.index(NT - 2) + 1)
                    act.wait_ge(x_loaded[t % XS], (b * 2 * NT // XS + t // XS + 1) * 16)
                    act.activation(feat[:, t, 0, :], x_in[:, t % XS, :], ACT.Copy,
                                   scale=dinv[:, t:t + 1]).then_inc(feat_hi, 1)
                else:
                    act.wait_ge(x1_ready, b * NT + t + 1)
                    act.copy(feat[:, t, 0, :], x1[:, t, :]).then_inc(feat_hi, 1)

            def split_unit(b, layer, j, u):
                if layer == 0 and u == 0:
                    act.wait_ge(transposed, b * NT + (TPC * (j + 1) if j < NJ - 1 else NT))
                if layer == 1 and u == 0:
                    act.wait_ge(eps_added, b * NT + TPC * (j + 1))
                act.wait_ge(unit_free, b * UNITS + RING + units_before(layer * LU + j * UPC + u))
                act.copy(ring_view(unit_hi, layer, j, u), at_unit(layer, j, u)).then_inc(hi_ready, 1)

            def split_agg(b, c):
                act.wait_ge(unit_free, b * UNITS + UPC * (c + 1) + RING)
                if 1 <= c <= NJ:
                    act.wait_ge(y_ready, b * NT + TPC * c)
                elif c:
                    act.wait_ge(agg_stored, (b * NJ + (c - NJ) + 1) * 16)
                if c == CPB - 1 or c == 0:
                    nb = b + 1 if c else b
                    if c == 0 or not (isinstance(b, int) and b == last_batch):
                        act.wait_ge(transposed, nb * NT + T_ORDER.index(NT - 1) + 1)
                        act.wait_ge(*sums(nb, NT - 1))
                if c == 0:
                    act.wait_ge(agg_stored, (b * NJ + 1) * 16)
                for ob in range(DK):
                    last = act.copy(agg[:, 0, ob, :], agg_ps[c % 2][ob][:, :])
                last.then_inc(agg_hi, 1)

            def store_agg(b, c):
                act.wait_ge(agg_lo, b * CPB + c + 3)
                act.dma_start(agg_scratch[b * NJ + (c - NJ)],
                              agg[:, :, :, :].bitcast(F32).rearrange("p h k n -> p (h k n)")).then_inc(agg_stored, 16)

            def scale_y(b, t):
                act.wait_ge(y_ready, b * NT + t + 1)
                act.wait_ge(y_used, b * NT + t + 1)
                act.activation(y_lo[:, t % 2, :], y_ps[t % TPC][:, D:2 * D], ACT.Copy,
                               scale=dinv[:, t:t + 1]).then_inc(ylo_ready, 1)

            def ahead(b):
                for u in range(AHEAD):
                    if u < AHEAD - 1:
                        split_unit(b, 0, 0, u)
                    for t in range(UT * u, UT * u + UT):
                        split_feat(b, 0, t)

            act.sem_inc(agg_stored, 16)
            act.wait_ge(consts_in, 5 * 16)
            act.copy(w0s[:, :, 0, :], w0_in).then_inc(w0_hi, 1)
            for k in range(NT):
                sum_rows(0, k, True)
            ahead(0)

            def body(b, is_last):
                split_unit(b, 0, 0, AHEAD - 1)
                for layer, j, u in steps():
                    c = layer * NJ + j
                    if c and u == 2:
                        split_agg(b, c - 1)
                    if c > NJ and u == 3:
                        store_agg(b, c - 1)
                    for t in scaled_at(layer, j, u):
                        scale_y(b, t)
                    for ly, t in feats_at(layer, j, u):
                        split_feat(b, ly, t)
                    split_unit(b, layer, j, u)
                    if layer and not is_last:
                        for k in summed_at(j, u):
                            sum_rows(b, k, False)
                    if is_last and c == CPB - 1 and u == 2:
                        act.wait_ge(w_in, 2 * 16)
                        wait_lo(act, b, LU + (NJ - 1) * UPC + 2)
                        act.copy(w1s[:, 0, :, :], w1_in).then_inc(w_hi, 1)
                        act.copy(w2s[:, :, 0, :], w2_in).then_inc(w_hi, 1)
                if not is_last:
                    for k in summed_at(NJ, 0):
                        sum_rows(b, k, False)
                    ahead(b + 1)
                split_agg(b, CPB - 1)
                store_agg(b, CPB - 1)

            over_batches(act, body)

        @block.gpsimd
        def _(pool):
            pool.memset(minus_half[:, :], -0.5)
            pool.memset(ln_eps[:, :], LN_EPS)
            pool.memset(fold[:, :], 0.0).then_inc(pool_consts, 1)
            pool.memset(ident[:, :], 0.0).then_inc(pool_consts, 1)
            pool.wait_ge(pool_consts, 2)
            pool.affine_select(out=ident[:, :], in_=ident[:, :], compare_op=ALU.not_equal, fill=1.0, base=0,
                               pattern=[[-1, P]], channel_multiplier=1).then_inc(pool_consts, 1)
            for n, s in enumerate(range(-(QUADS - 1), QUADS)):
                if n:
                    pool.wait_ge(pool_consts, 3 + n)
                pool.affine_select(out=fold[:, :], in_=fold[:, :], compare_op=ALU.not_equal, fill=1.0,
                                   base=-QP * s, pattern=[[-1, P]], channel_multiplier=1).then_inc(pool_consts, 1)
            pool.wait_ge(consts_in, 5 * 16)

            def invert(b):
                pool.wait_ge(deg_ready, b + 1)
                for cols in (slice(0, TPC), slice(TPC, NT)):
                    pool.tensor_tensor(dinv[:, cols], deg[:, cols], minus_half[:, cols], ALU.pow)\
                        .then_inc(dinv_ready, 1)

            invert(0)

            def body(b, is_last):
                for j in range(NJ):
                    for i in range(TPC):
                        t = TPC * j + i
                        pool.wait_ge(x_loaded[t % XS], (b * 2 * NT // XS + NT // XS + t // XS + 1) * 16)
                        pool.tensor_tensor(x_in[:, t % XS, :], x_in[:, t % XS, :], bias[:, :], ALU.add)\
                            .then_inc(biased, 1)
                    pool.wait_ge(var_ready, b * NJ + j + 1)
                    pool.tensor_tensor(var_eps[:, :], mean_var[:, :, 1], ln_eps[:, :], ALU.add).then_inc(veps_ready, 1)
                    pool.wait_ge(veps_ready, b * NJ + j + 1)
                    pool.tensor_tensor(rstd[:, :], var_eps[:, :], minus_half[:, 0:TPC], ALU.pow)\
                        .then_inc(rstd_ready, 1)
                for j in range(1, NJ):
                    for u in POOL_UNITS:
                        pool.wait_ge(hi_ready, b * UNITS + LU + j * UPC + u + 1)
                        pool.tensor_tensor(ring_view(unit_lo, 1, j, u), at_unit(1, j, u),
                                           ring_view(unit_hi, 1, j, u).bitcast(F32),
                                           ALU.subtract).then_inc(pool_lo, 1)
                if not is_last:
                    invert(b + 1)

            over_batches(pool, body)

        @block.vector
        def _(dve):
            dve.sem_inc(summed, 1)
            dve.sem_inc(y_used, 2)
            dve.sem_inc(agg_lo, 2)

            def transpose_rows(b, k, first):
                if first is None:
                    dve.wait_ge(*last_rows_here(b, k))
                else:
                    dve.wait_ge(*rows_here(b, k, first))
                src = rows_view(k, first).rearrange("p q (t c) -> p q t c", c=QP)
                dst = at[:, :, k * P:(k + 1) * P].rearrange("p t (q a) -> p q t a", a=QP)
                dve.transpose(dst, src).then_inc(transposed, 1)

            def sum_rows(b, k, first):
                if k not in DVE_SUMS:
                    return
                dve.wait_ge(*rows_here(b, k, first))
                dve.tensor_reduce(part[:, k, :], rows_view(k, first), axis=mybir.AxisListType.X, op=ALU.add)\
                    .then_inc(dve_summed, 1)

            def split_feat(b, layer, t):
                dve.wait_ge(feat_hi, b * 2 * NT + layer * NT + t + 1)
                hi = feat[:, t, 0, :].bitcast(F32)
                if layer == 0:
                    last = dve.scalar_tensor_tensor(feat[:, t, 1, :], x_in[:, t % XS, :], dinv[:, t:t + 1], hi,
                                                    op0=ALU.mult, op1=ALU.subtract)
                    last.then_inc(feat_lo, 1)
                else:
                    dve.tensor_tensor(feat[:, t, 1, :], x1[:, t, :], hi, ALU.subtract).then_inc(feat_lo, 1)

            def split_unit(b, layer, j, u):
                if pool_splits(layer, j, u):
                    return
                dve.wait_ge(hi_ready, b * UNITS + layer * LU + j * UPC + u + 1)
                dve.tensor_tensor(ring_view(unit_lo, layer, j, u), at_unit(layer, j, u),
                                  ring_view(unit_hi, layer, j, u).bitcast(F32),
                                  ALU.subtract).then_inc(dve_lo, 1)

            def find_deg(b):
                dve.wait_ge(sums_folded, b + 1)
                folded = fold_ps[:, 0:NT * QUADS].rearrange("p (t q) -> p t q", q=QUADS)
                for q in range(QUADS):
                    rows = slice(q * QP, (q + 1) * QP)
                    last = dve.tensor_scalar(deg[rows, :], folded[rows, :, q], DEG_EPS, None, op0=ALU.add)
                last.then_inc(deg_ready, 1)

            dve.wait_ge(w0_hi, 1)
            dve.tensor_tensor(w0s[:, :, 1, :], w0_in, w0s[:, :, 0, :].bitcast(F32), ALU.subtract)\
                .then_inc(w0_ready, 1)
            for k in range(NT - TPC):
                sum_rows(0, k, True)
                transpose_rows(0, k, True)
            for k in range(NT - TPC, NT):
                sum_rows(0, k, True)
            for k in T_ORDER[NT - TPC:NT - len(LATE_T)]:
                transpose_rows(0, k, True)
            find_deg(0)
            for u in range(AHEAD):
                if u < AHEAD - 1:
                    split_unit(0, 0, 0, u)
                for t in range(UT * u, UT * u + UT):
                    split_feat(0, 0, t)

            def body(b, is_last):
                def split_agg(c):
                    dve.wait_ge(agg_hi, b * CPB + c + 1)
                    for ob in range(DK):
                        last = dve.tensor_tensor(agg[:, 1, ob, :], agg_ps[c % 2][ob][:, :],
                                                 agg[:, 0, ob, :].bitcast(F32), ALU.subtract)
                    last.then_inc(agg_lo, 1)

                def add_up(t):
                    dve.wait_ge(ylo_ready, b * NT + t + 1)
                    dve.scalar_tensor_tensor(x1[:, t, :], y_ps[t % TPC][:, 0:D], dinv[:, t:t + 1], y_lo[:, t % 2, :],
                                             op0=ALU.mult, op1=ALU.add).then_inc(y_used, 1)
                    dve.wait_ge(biased, b * NT + t + 1)
                    dve.wait_ge(y_used, b * NT + t + 3)
                    last = dve.tensor_tensor(x1[:, t, :], x1[:, t, :], x_in[:, t % XS, :], ALU.add)
                    last.then_inc(summed, 1)
                    dve.wait_ge(summed, b * NT + t + 2)
                    dve.bn_stats(stats[:, :], x1[:, t, :]).then_inc(stats_done, 1)
                    dve.wait_ge(stats_done, b * NT + t + 1)
                    dve.memset(wait_here[:, :], 0.0)
                    last = dve.bn_aggr(mean_var[:, t % TPC, :], stats[:, :])
                    if t % TPC == TPC - 1:
                        last.then_inc(var_ready, 1)

                def normalise(j):
                    dve.wait_ge(rstd_ready, b * NJ + j + 1)
                    for i in range(TPC):
                        t = TPC * j + i
                        dve.tensor_scalar(x1[:, t, :], x1[:, t, :], mean_var[:, i, 0:1], rstd[:, i:i + 1],
                                          op0=ALU.subtract, op1=ALU.mult).then_inc(x1_ready, 1)

                def add_eps(j):
                    for t in range(TPC * j, TPC * (j + 1)):
                        diag = at[:, t, t * P:(t + 1) * P]
                        dve.scalar_tensor_tensor(diag, ident[:, :], eps_sb[:, 0:1], diag, op0=ALU.mult,
                                                 op1=ALU.add).then_inc(eps_added, 1)

                def columns_free(j):
                    wait_lo(dve, b, LU + UPC * (j + 1))

                split_unit(b, 0, 0, AHEAD - 1)
                for layer, j, u in steps():
                    c = layer * NJ + j
                    if (layer == 0 and j or c == NJ) and u == 3:
                        add_eps(j - 1 if layer == 0 else NJ - 1)
                    if c and u == 2:
                        split_agg(c - 1)
                    for t in scaled_at(layer, j, u):
                        add_up(t)
                    for i in normalised_at(layer, j, u):
                        normalise(i)
                    for ly, t in feats_at(layer, j, u):
                        split_feat(b, ly, t)
                    split_unit(b, layer, j, u)
                    if c == 0 and 3 <= u < 3 + len(LATE_T):
                        transpose_rows(b, LATE_T[u - 3], None)
                    if is_last and c == CPB - 1 and u == 4:
                        dve.wait_ge(w_hi, 1)
                        dve.tensor_tensor(w1s[:, 1, :, :], w1_in, w1s[:, 0, :, :].bitcast(F32), ALU.subtract)\
                            .then_inc(w_ready, 1)
                        dve.wait_ge(w_hi, 2)
                        dve.tensor_tensor(w2s[:, :, 1, :], w2_in, w2s[:, :, 0, :].bitcast(F32), ALU.subtract)\
                            .then_inc(w_ready, 1)
                    if layer and not is_last:
                        for k in summed_at(j, u):
                            sum_rows(b, k, False)
                        for k in transposed_at(j, u):
                            if k % TPC == 0:
                                columns_free(k // TPC)
                            transpose_rows(b, k, False)
                if not is_last:
                    columns_free(NJ - 1)
                    for k, what in TAIL:
                        if what == "S":
                            sum_rows(b, k, False)
                        elif what == "T":
                            transpose_rows(b, k, False)
                        elif what == "U":
                            split_unit(b + 1, 0, 0, k)
                        elif what == "P":
                            for t in range(UT * k, UT * k + UT):
                                split_feat(b + 1, 0, t)
                        else:
                            find_deg(b + 1)
                split_agg(CPB - 1)

            over_batches(dve, body)

        @block.tensor
        def _(pe):
            pe.sem_inc(unit_free, RING)
            pe.wait_ge(w0_ready, 1)
            pe.wait_ge(pool_consts, 3 + 2 * QUADS - 1)

            def fold_sums(b):
                pe.wait_ge(act_summed, (b + 1) * ACT_TILES)
                pe.wait_ge(dve_summed, (b + 1) * len(DVE_SUMS))
                pe.wait_ge(y_used, b * NT + 2)
                pe.matmul(fold_ps[:, 0:NT * QUADS], fold[:, :], part[:, :, :].rearrange("p t q -> p (t q)"),
                          start=True, stop=True).then_inc(sums_folded, 1)

            fold_sums(0)

            def body(b, is_last):
                def times_w(j):
                    pe.wait_ge(agg_lo, b * CPB + j + 3)
                    if j == 0:
                        pe.wait_ge(deg_ready, b + 1)
                    pe.wait_ge(y_used, b * NT + TPC * j + 2)
                    for i in range(TPC):
                        cols = slice(i * P, (i + 1) * P)
                        for k in range(DK):
                            pe.matmul(y_ps[i][:, :], agg[:, 0, k, cols], w0s[:, k, :, :].rearrange("p h d -> p (h d)"),
                                      start=(k == 0), stop=False)
                            last = pe.matmul(y_ps[i][:, 0:D], agg[:, 1, k, cols], w0s[:, k, 0, :],
                                             start=False, stop=(k == DK - 1))
                        last.then_inc(y_ready, 1)

                for layer in range(2):
                    for j in range(NJ):
                        c = layer * NJ + j
                        for u in range(UPC):
                            if u == (1 if c == NJ else 2) and 1 <= c <= NJ:
                                times_w(c - 1)
                            if c == CPB - 1 and u == FOLD_U and not is_last:
                                fold_sums(b + 1)
                            if u == 0:
                                pe.wait_ge(agg_lo, b * CPB + c + 1)
                            n = layer * LU + j * UPC + u + 1
                            if pool_splits(layer, j, u):
                                pe.wait_ge(pool_lo, b * POOL_TOTAL + pool_units(n))
                            else:
                                pe.wait_ge(dve_lo, b * (UNITS - POOL_TOTAL) + n - pool_units(n))
                            if j == 0:
                                pe.wait_ge(feat_lo, b * 2 * NT + layer * NT + UT * (u + 1))
                            hi, lo = ring_view(unit_hi, layer, j, u), ring_view(unit_lo, layer, j, u)
                            for tt in range(UT):
                                t = UT * u + tt
                                for ob in range(DK):
                                    out = agg_ps[c % 2][ob][:, :]
                                    f_hi = feat[:, t, 0, ob * P:(ob + 1) * P]
                                    f_lo = feat[:, t, 1, ob * P:(ob + 1) * P]
                                    pe.matmul(out, f_hi, hi[:, tt, :], start=(t == 0), stop=False)
                                    pe.matmul(out, f_hi, lo[:, tt, :], start=False, stop=False)
                                    last = pe.matmul(out, f_lo, hi[:, tt, :], start=False, stop=(t == NT - 1))
                            last.then_inc(unit_free, 1)
                if FOLD_U == 8 and not is_last:
                    fold_sums(b + 1)

            over_batches(pe, body)


def dense(nc, g):
    B, D, H, CH, NJ, TPC, DK, HK = (g[k] for k in ("B", "D", "H", "CH", "NJ", "TPC", "DK", "HK"))
    agg_scratch, x1_scratch, y_rows = g["agg_scratch"], g["x1_scratch"], g["y_rows"]
    ident, psum, in_at, w1s, w2s, agg_in, b1_sb, rms_sb, agg_stored, agg_here, w_ready = (
        g[k] for k in ("ident", "psum", "in_at", "w1s", "w2s", "agg_in", "b1_sb", "rms_sb", "agg_stored", "agg_here",
                       "w_ready"))
    NC = B * NJ

    with ExitStack() as ctx:
        def sb(name, shape, dt=F32):
            return ctx.enter_context(nc.sbuf_tensor(name, shape, dt))

        def sem(name):
            return ctx.enter_context(nc.semaphore(name))

        b2_sb = sb("b2_sb", [P, D])
        ones = sb("ones", [P, P])
        minus_half4 = sb("minus_half4", [P, TPC])
        wait_here2 = sb("wait_here2", [P, 1])
        ln_eps4 = sb("ln_eps4", [P, TPC])
        x1_in = sb("x1_in", [P, 2, TPC, D])
        hid = in_at("hid", [P, 2, HK, CH], 10)
        s_hi = in_at("s_hi", [P, HK, CH], 6, F32R)
        s_lo = in_at("s_lo", [P, HK, CH], 8, F32R)
        sq = in_at("sq", [P, HK, CH], 14)
        sum_sq = sb("sum_sq", [P, 2, CH])
        mean_sq = sb("mean_sq", [P, TPC])
        rms_inv = sb("rms_inv", [P, TPC])
        diag = sb("diag", [P, CH])
        out = sb("out", [P, 2, TPC, D])
        bstats = sb("bstats", [P, TPC, 6])
        mv = sb("mv", [P, TPC, 2])
        vare = sb("vare", [P, TPC])
        rstd2 = sb("rstd2", [P, TPC])

        h_ps = psum[0:2]
        o_ps = psum[2:6]
        sq_ps = psum[6]
        r_ps = psum[7]

        b2_in = sem("b2_in")
        ones_set = sem("ones_set")
        x1_here = [sem(f"x1_here{s}") for s in range(2)]
        h_done = sem("h_done")
        h_ready = sem("h_ready")
        squared = sem("squared")
        sq_added = sem("sq_added")
        sq_summed = sem("sq_summed")
        mean_ready = sem("mean_ready")
        rms_ready = sem("rms_ready")
        diag_ready = sem("diag_ready")
        r_spread = sem("r_spread")
        z_ready = sem("z_ready")
        act_ready = sem("act_ready")
        shi_ready = sem("shi_ready")
        slo_ready = sem("slo_ready")
        w2_done = sem("w2_done")
        x1_biased = sem("x1_biased")
        half_added = sem("half_added")
        o_read = sem("o_read")
        o_stats = sem("o_stats")
        o_var = sem("o_var")
        vare_ready = sem("vare_ready")
        rstd2_ready = sem("rstd2_ready")
        out_ready = sem("out_ready")
        out_stored = [sem(f"out_stored{s}") for s in range(2)]
        block = ctx.enter_context(nc.Block())

        def wait(eng, semaphore, value):
            if not isinstance(value, int) or value > 0:
                eng.wait_ge(semaphore, value)

        def over_steps(eng, step):
            for o in range(NJ):
                step(0, o)
            if B > 2:
                with eng.Fori(1, B) as m:
                    for o in range(NJ):
                        step(m, o)
            elif B == 2:
                for o in range(NJ):
                    step(1, o)
            for o in range(3):
                step(B, o)

        def there(m, o, back):
            if isinstance(m, int):
                return 0 <= NJ * m + o - back < NC
            return True

        def used(m, o):
            return m * (NJ // 2) + o // 2

        @block.sync
        def _(sp):
            sp.dma_start(b2_sb[:, :], g["b2"].to_broadcast([P, D])).then_inc(b2_in, 16)

            def load_agg(m, o):
                src = agg_scratch[NJ * m + o]
                waits = (agg_stored, (NJ * m + o + 2) * 16), (h_done, (NJ * m + o - 1) * HK)
                values = [v if isinstance(v, int) else sp.to_reg(v) for _, v in waits]
                for (semaphore, _), value in zip(waits, values):
                    wait(sp, semaphore, value)
                sp.dma_start(agg_in[:, o % 2, :, :, :].bitcast(F32).rearrange("p h k n -> p (h k n)"),
                             src).then_inc(agg_here[o % 2], 16)

            def step(m, o):
                if there(m, o, 0) and not (isinstance(m, int) and m == 0 and o < 2):
                    load_agg(m, o)
                if there(m, o, 2):
                    wait(sp, half_added, (NJ * m + o - 3) * TPC)
                    sp.dma_start(x1_in[:, o % 2, :, :].rearrange("p t d -> p (t d)"),
                                 x1_scratch[NJ * m + o - 2]).then_inc(x1_here[o % 2], 16)
                if there(m, o, 3):
                    b, j = (m, o - 3) if o >= 3 else (m - 1, o - 3 + NJ)
                    for t in range(TPC):
                        wait(sp, out_ready, (NJ * m + o - 3) * TPC + t + 1)
                        sp.dma_start(y_rows[b, TPC * j + t], out[:, (o - 3) % 2, t, :])\
                            .then_inc(out_stored[(o - 3) % 2], 16)

            over_steps(sp, step)
            for s in range(2):
                sp.wait_ge(out_stored[s], NC // 2 * TPC * 16)

        @block.scalar
        def _(act):
            def activate(m, o, h):
                n = (NJ * m + o) * HK + h
                cur = hid[:, o % 2, h, :]
                act.wait_ge(z_ready, n + 1)
                act.activation(cur, cur, ACT.Silu, scale=rms_sb[:, h:h + 1]).then_inc(act_ready, 1)
                act.wait_ge(act_ready, n + 1)
                wait(act, w2_done, n - HK + 1)
                act.copy(s_hi[:, h, :], cur).then_inc(shi_ready, 1)

            def square(m, o, h):
                i = NJ * m + o
                act.wait_ge(h_ready, i * HK + h + 1)
                if h == 0:
                    wait(act, sq_summed, i - 1)
                else:
                    wait(act, sq_added, (i - 1) * (HK - 1) + h)
                dst = sq[:, h, :] if h else sum_sq[:, o % 2, :]
                act.activation(dst, hid[:, o % 2, h, :], ACT.Square).then_inc(squared, 1)

            def step(m, o):
                i = NJ * m + o
                if there(m, o, 0):
                    for h in range(HK):
                        act.wait_ge(h_done, i * HK + h + 1)
                        wait(act, slo_ready, (i - 2) * HK + h + 1)
                        act.activation(hid[:, o % 2, h, :], h_ps[h % 2][:, :], ACT.Identity,
                                       bias=b1_sb[:, h:h + 1]).then_inc(h_ready, 1)
                        if h:
                            square(m, o, h - 1)
                    square(m, o, HK - 1)
                if there(m, o, 1):
                    for h in range(HK):
                        activate(m, o - 1, h)

            over_steps(act, step)

        @block.gpsimd
        def _(pool):
            pool.memset(ones[:, :], 1.0).then_inc(ones_set, 1)
            pool.memset(minus_half4[:, :], -0.5).then_inc(ones_set, 1)
            pool.memset(ln_eps4[:, :], LN_EPS).then_inc(ones_set, 1)
            pool.wait_ge(ones_set, 3)
            pool.wait_ge(b2_in, 16)

            def add_square(m, o, h):
                i = NJ * m + o
                pool.wait_ge(squared, i * HK + h + 1)
                wait(pool, sq_added, i * (HK - 1) + h - 1)
                pool.tensor_tensor(sum_sq[:, o % 2, :], sum_sq[:, o % 2, :], sq[:, h, :], ALU.add)\
                    .then_inc(sq_added, 1)

            def step(m, o):
                i = NJ * m + o
                if there(m, o, 1):
                    pool.wait_ge(mean_ready, i)
                    pool.tensor_tensor(rms_inv[:, :], mean_sq[:, :], minus_half4[:, :], ALU.pow).then_inc(rms_ready, 1)
                if there(m, o, 0):
                    for h in (1, 2):
                        add_square(m, o, h)
                if there(m, o, 3):
                    pool.wait_ge(o_var, i - 2)
                    pool.tensor_tensor(vare[:, :], mv[:, :, 1], ln_eps4[:, :], ALU.add).then_inc(vare_ready, 1)
                    pool.wait_ge(vare_ready, i - 2)
                    pool.tensor_tensor(rstd2[:, :], vare[:, :], minus_half4[:, :], ALU.pow).then_inc(rstd2_ready, 1)
                if there(m, o, 0):
                    for h in range(3, HK):
                        add_square(m, o, h)
                if there(m, o, 2):
                    p = o % 2
                    pool.wait_ge(x1_here[p], (used(m, o - 2) + 1) * 16)
                    for t in range(TPC):
                        pool.tensor_tensor(x1_in[:, p, t, :], x1_in[:, p, t, :], b2_sb[:, :], ALU.add)\
                            .then_inc(x1_biased, 1)

            over_steps(pool, step)

        @block.vector
        def _(dve):
            def scale(m, o, h):
                cur = hid[:, o % 2, h, :]
                if h == 0:
                    dve.wait_ge(r_spread, NJ * m + o + 1)
                dve.tensor_tensor(cur, cur, r_ps[:, :], ALU.mult).then_inc(z_ready, 1)

            def split(m, o, h):
                dve.wait_ge(shi_ready, (NJ * m + o) * HK + h + 1)
                dve.tensor_tensor(s_lo[:, h, :], hid[:, o % 2, h, :], s_hi[:, h, :].bitcast(F32), ALU.subtract)\
                    .then_inc(slo_ready, 1)

            def add_up(m, o, t):
                n = (NJ * m + o) * TPC + t
                v = out[:, o % 2, t, :]
                if t == 0:
                    dve.wait_ge(w2_done, (NJ * m + o + 1) * HK)
                    wait(dve, out_stored[o % 2], used(m, o) * TPC * 16)
                dve.wait_ge(x1_biased, n + 1)
                dve.tensor_tensor(v, o_ps[t][:, 0:D], x1_in[:, o % 2, t, :], ALU.add).then_inc(half_added, 1)
                dve.wait_ge(half_added, n + 1)
                dve.tensor_tensor(v, v, o_ps[t][:, D:2 * D], ALU.add).then_inc(o_read, 1)
                dve.wait_ge(o_read, n + 1)
                dve.bn_stats(bstats[:, t, :], v).then_inc(o_stats, 1)
                dve.wait_ge(o_stats, n + 1)
                dve.memset(wait_here2[:, :], 0.0)
                last = dve.bn_aggr(mv[:, t, :], bstats[:, t, :])
                if t == TPC - 1:
                    last.then_inc(o_var, 1)

            def step(m, o):
                i = NJ * m + o
                if there(m, o, 3):
                    add_up(m, o - 3, 0)
                if there(m, o, 1):
                    dve.wait_ge(sq_summed, i)
                    dve.tensor_scalar(mean_sq[:, :], sq_ps[:, 0:TPC], 1.0 / H, RMS_EPS, op0=ALU.mult,
                                      op1=ALU.add).then_inc(mean_ready, 1)
                if there(m, o, 3):
                    add_up(m, o - 3, 1)
                if there(m, o, 1):
                    dve.wait_ge(rms_ready, i)
                    wait(dve, r_spread, i - 1)
                    for t in range(TPC):
                        last = dve.tensor_scalar(diag[:, t * P:(t + 1) * P], ident[:, :], rms_inv[:, t:t + 1], None,
                                                 op0=ALU.mult)
                    last.then_inc(diag_ready, 1)
                if there(m, o, 3):
                    add_up(m, o - 3, 2)
                    add_up(m, o - 3, 3)
                if there(m, o, 1):
                    for h in range(2):
                        scale(m, o - 1, h)
                if there(m, o, 3):
                    dve.wait_ge(rstd2_ready, i - 2)
                    for t in range(TPC):
                        v = out[:, (o - 3) % 2, t, :]
                        dve.tensor_scalar(v, v, mv[:, t, 0:1], rstd2[:, t:t + 1], op0=ALU.subtract,
                                          op1=ALU.mult).then_inc(out_ready, 1)
                if there(m, o, 1):
                    for h in range(2, HK):
                        scale(m, o - 1, h)
                        split(m, o - 1, h - 2)
                    for h in (HK - 2, HK - 1):
                        split(m, o - 1, h)

            over_steps(dve, step)

        @block.tensor
        def _(pe):
            pe.wait_ge(ones_set, 3)

            def sum_squares(m, o):
                i = NJ * m + o
                pe.wait_ge(sq_added, (i + 1) * (HK - 1))
                wait(pe, mean_ready, i)
                for t in range(TPC):
                    last = pe.matmul(sq_ps[:, t:t + 1], sum_sq[:, o % 2, t * P:(t + 1) * P], ones[:, 0:1],
                                     start=True, stop=True)
                last.then_inc(sq_summed, 1)

            def spread_rms(m, o):
                i = NJ * m + o
                pe.wait_ge(diag_ready, i + 1)
                wait(pe, z_ready, i * HK)
                pe.matmul(r_ps[:, :], ones[:, :], diag[:, :], start=True, stop=True).then_inc(r_spread, 1)

            def step(m, o):
                i = NJ * m + o
                if there(m, o, 0):
                    pe.wait_ge(agg_here[o % 2], (used(m, o) + 1) * 16)
                    if isinstance(m, int) and m == 0 and o == 0:
                        pe.wait_ge(w_ready, 1)
                    a_hi = agg_in[:, o % 2, 0, :, :]
                    a_lo = agg_in[:, o % 2, 1, :, :]
                for h in range(HK):
                    if there(m, o, 0):
                        wait(pe, h_ready, i * HK + h - 1)
                        bank = h_ps[h % 2][:, :]
                        cols = slice(h * P, (h + 1) * P)
                        for k in range(DK):
                            pe.matmul(bank, w1s[:, 0, k, cols], a_hi[:, k, :], start=(k == 0), stop=False)
                            pe.matmul(bank, w1s[:, 0, k, cols], a_lo[:, k, :], start=False, stop=False)
                            last = pe.matmul(bank, w1s[:, 1, k, cols], a_hi[:, k, :], start=False, stop=(k == DK - 1))
                        last.then_inc(h_done, 1)
                    if there(m, o, 1) and h == 1:
                        sum_squares(m, o - 1)
                    if there(m, o, 1) and h == 5:
                        spread_rms(m, o - 1)
                if there(m, o, 2):
                    wait(pe, o_read, (i - 2) * TPC)
                    if isinstance(m, int) and i == 2:
                        pe.wait_ge(w_ready, 2)
                    for h in range(HK):
                        pe.wait_ge(slo_ready, (i - 2) * HK + h + 1)
                        for t in range(TPC):
                            cols = slice(t * P, (t + 1) * P)
                            pe.matmul(o_ps[t][:, :], s_hi[:, h, cols], w2s[:, h, :, :].rearrange("p s d -> p (s d)"),
                                      start=(h == 0), stop=False)
                            last = pe.matmul(o_ps[t][:, 0:D], s_lo[:, h, cols], w2s[:, h, 0, :],
                                             start=False, stop=(h == HK - 1))
                        last.then_inc(w2_done, 1)

            over_steps(pe, step)


_OUT = ((8, 2048, 256), "float32")


def kernel(x, adj, L0_gnn_weight, L0_gnn_bias, L1_gnn_epsilon, L1_gnn_W1, L1_gnn_b1, L1_gnn_rms_weight, L1_gnn_W2,
           L1_gnn_b2):
    import numpy as np
    import concourse.bacc as bacc
    from concourse.bass_utils import run_bass_kernel_spmd

    nc = bacc.Bacc("TRN2", target_bir_lowering=False, num_devices=1, dynamic_dma_scratch_size=1024)
    arrays = {
        "x": np.asarray(x),
        "adj": np.asarray(adj),
        "w0": np.asarray(L0_gnn_weight),
        "bias0": np.asarray(L0_gnn_bias).reshape(1, -1),
        "eps": np.asarray(L1_gnn_epsilon).reshape(1, 1),
        "w1": np.asarray(L1_gnn_W1),
        "b1": np.asarray(L1_gnn_b1),
        "rms_w": np.asarray(L1_gnn_rms_weight),
        "w2": np.asarray(L1_gnn_W2),
        "b2": np.asarray(L1_gnn_b2).reshape(1, -1),
    }
    args = {n: nc.dram_tensor(n, a.shape, mybir.dt.from_np(a.dtype), kind="ExternalInput").ap()
            for n, a in arrays.items()}
    y = nc.dram_tensor("y", _OUT[0], F32, kind="ExternalOutput").ap()
    build(nc, **args, y=y)
    results = run_bass_kernel_spmd(nc, [arrays], core_ids=[0]).results
    return results[0]["y"]
```

```python
from contextlib import ExitStack

import concourse.bass as bass
from concourse import mybir

F32 = mybir.dt.float32
F32R = mybir.dt.float32r
ALU = mybir.AluOpType
ACT = mybir.ActivationFunctionType
P = 128
QUADS = 4
QP = P // QUADS
LN_EPS = 1e-5
DEG_EPS = 1e-5
RMS_EPS = 1e-6
FILL = 2
TAIL_SPREAD = 0


def build(nc, x, adj, w0, bias0, eps, w1, b1, rms_w, w2, b2, y):
    B, N, D = x.shape
    H = w1.shape[1]
    NT = N // P
    CH = 512
    NJ = N // CH
    TPC = CH // P
    DK = D // P
    HK = H // P
    QW = N // QUADS
    UT = 2
    UPC = NT // UT
    UNITS = 2 * NJ * UPC
    RING = 3
    assert D == 256 and QW == CH and UPC == 8 and TPC == QUADS and DK == 2

    adj_rows = adj.rearrange("b (Q k a) (q f) -> b k Q q a f", Q=QUADS, a=QP, q=QUADS)
    x_rows = x.rearrange("b (q t c) d -> b t q c d", q=QUADS, c=QP)
    y_rows = y.rearrange("b (q t c) d -> b t q c d", q=QUADS, c=QP)
    agg_scratch = nc.dram_tensor("agg_scratch", [B * NJ, P, 2 * DK * CH], F32)
    x1_scratch = nc.dram_tensor("x1_scratch", [B * NJ, P, TPC * D], F32)

    with ExitStack() as both:
        def keep(name, shape, dt=F32):
            return both.enter_context(nc.sbuf_tensor(name, shape, dt))

        def keep_sem(name):
            return both.enter_context(nc.semaphore(name))

        ident = keep("ident", [P, P])
        at_offset = nc.sbuf_base
        at = keep("at", [P, NT, N])

        def in_at(name, shape, block, dt=F32):
            return nc.alloc_sbuf_tensor_at(name, shape, dt, offset=at_offset + block * N * 4)

        w1s = in_at("w1s", [P, 2, DK, H], 0, F32R)
        w2s = in_at("w2s", [P, HK, 2, D], 2, F32R)
        agg_in = in_at("agg_in", [P, 2, 2, DK, CH], 4, F32R)
        stage = keep("stage", [P, 2, QUADS, CH])
        agg_offset = nc.sbuf_base
        agg = keep("agg", [P, 2, DK, CH], F32R)
        agg_rows = nc.alloc_sbuf_tensor_at("agg_rows", [P, QUADS, CH], F32, offset=agg_offset)
        b1_sb = keep("b1_sb", [P, HK])
        rms_sb = keep("rms_sb", [P, HK])
        agg_stored = keep_sem("agg_stored")
        agg_here = [keep_sem(f"agg_here{s}") for s in range(2)]
        w_ready = keep_sem("w_ready")
        psum = [both.enter_context(nc.psum_tensor(f"bank{i}", [P, CH], F32)) for i in range(8)]

        shared = locals()
        aggregate(nc, shared)
        dense(nc, shared)


SHIFTS = (9, 25)
POOL_UNITS = ((), (0, 1, 2, 5), (0, 1, 7), (0, 1, 7))
DVE_SUMS = (13,)
SUM_AT = {(0, 7): [0], (1, 1): [1], (1, 2): [2], (1, 4): [3], (1, 5): [4], (1, 7): [5], (2, 1): [6], (2, 4): [7],
          (2, 5): [8], (2, 7): [9], (3, 2): [10], (3, 3): [11], (3, 4): [12], (3, 6): [13], (3, 7): [14, 15]}
T_AT = {(1, 1): [0, 1], (1, 2): [2], (1, 4): [3], (2, 0): [4], (2, 1): [5, 6], (2, 5): [7], (3, 0): [8, 9],
        (3, 2): [10, 11]}
LATE_T_AT = {(0, 7): [12], (1, 1): [13]}
T_ORDER = [*range(12), 14, 15, 12, 13]
LOAD_X = 12
PAIRS_AT = {2: [4], 3: [5], 7: [6, 7]}


def aggregate(nc, g):
    B, N, D, NT, CH, NJ, TPC, DK, UT, UPC, UNITS, RING = (
        g[k] for k in ("B", "N", "D", "NT", "CH", "NJ", "TPC", "DK", "UT", "UPC", "UNITS", "RING"))
    adj_rows, x_rows, agg_scratch, x1_scratch = (
        g[k] for k in ("adj_rows", "x_rows", "agg_scratch", "x1_scratch"))
    ident, psum, at, w1s, w2s, stage, agg_in, agg, agg_rows = (
        g[k] for k in ("ident", "psum", "at", "w1s", "w2s", "stage", "agg_in", "agg", "agg_rows"))
    b1_sb, rms_sb, agg_stored, agg_here, w_ready = (
        g[k] for k in ("b1_sb", "rms_sb", "agg_stored", "agg_here", "w_ready"))
    last_batch = B - 1
    CPB = 2 * NJ
    LU = NJ * UPC
    XF = 8
    XS = 4
    assert (UNITS + len(SHIFTS)) % RING == 0
    AHEAD = RING

    with ExitStack() as ctx:
        def sb(name, shape, dt=F32):
            return ctx.enter_context(nc.sbuf_tensor(name, shape, dt))

        def sem(name):
            return ctx.enter_context(nc.semaphore(name))

        feat_offset = nc.sbuf_base
        feat = sb("feat", [P, NT, 2, D], F32R)
        x1 = stage[:, :, :, :].rearrange("p s q f -> p (s q f)").rearrange("p (t d) -> p t d", d=D)
        unit_hi = sb("unit_hi", [P, RING, UT * CH], F32R)
        unit_lo = sb("unit_lo", [P, RING, UT * CH], F32R)
        w0s = sb("w0s", [P, DK, 2, D], F32R)
        fold = sb("fold", [P, P])
        bias = sb("bias", [P, D])
        eps_sb = sb("eps_sb", [P, 1])
        third = sb("third", [P, QUADS, CH])
        x_in = third[:, :, :].rearrange("p q (s d) -> p (q s) d", d=D)
        y_lo = third[:, 2, :].rearrange("p (s d) -> p s d", d=D)
        part = sb("part", [P, NT, QUADS])
        deg = sb("deg", [P, NT])
        dinv = sb("dinv", [P, NT])
        minus_half = sb("minus_half", [P, NT])
        wait_here = sb("wait_here", [P, 1])
        ln_eps = sb("ln_eps", [P, TPC])
        stats = sb("stats", [P, 6])
        mean_var = sb("mean_var", [P, TPC, 2])
        var_eps = sb("var_eps", [P, TPC])
        rstd = sb("rstd", [P, TPC])
        w0_in = x_in[:, 0:DK, :]
        w1_in = stage[:, 0, :, :].rearrange("p (k i) n -> p k (i n)", k=DK)
        w2_in = stage[:, 1, :, :].rearrange("p q (i d) -> p (q i) d", d=D)

        agg_ps = [[psum[2 * s + ob] for ob in range(DK)] for s in range(2)]
        y_ps = psum[4:8]
        fold_ps = psum[7]

        places = [stage[:, 0, :, :], stage[:, 1, :, :],
                  nc.alloc_sbuf_tensor_at("feat_rows", [P, QUADS, CH], F32, offset=feat_offset)[:, :, :],
                  agg_rows[:, :, :], third[:, :, :]]
        FEAT_PLACE, AGG_PLACE, THIRD_PLACE = 2, 3, 4
        FIRST_PLACES = [0, 1, FEAT_PLACE, AGG_PLACE] * (NT // 4)
        LATER_PLACES = [0, THIRD_PLACE, 1] * 3 + [0, THIRD_PLACE, 1, 0, 1, FEAT_PLACE, AGG_PLACE]

        rows_in = [sem(f"rows_in{s}") for s in range(len(places))]
        x_loaded = [sem(f"x_loaded{s}") for s in range(XF)]
        consts_in = sem("consts_in")
        pool_consts = sem("pool_consts")
        w0_hi = sem("w0_hi")
        w0_ready = sem("w0_ready")
        act_summed = sem("act_summed")
        dve_summed = sem("dve_summed")
        transposed = sem("transposed")
        sums_folded = sem("sums_folded")
        deg_ready = sem("deg_ready")
        dinv_ready = sem("dinv_ready")
        hi_ready = sem("hi_ready")
        dve_lo = sem("dve_lo")
        pool_lo = sem("pool_lo")
        unit_free = sem("unit_free")
        feat_hi = sem("feat_hi")
        feat_lo = sem("feat_lo")
        agg_hi = sem("agg_hi")
        agg_lo = sem("agg_lo")
        w_in = sem("w_in")
        w_hi = sem("w_hi")
        y_ready = sem("y_ready")
        ylo_ready = sem("ylo_ready")
        y_used = sem("y_used")
        biased = sem("biased")
        summed = sem("summed")
        stats_done = sem("stats_done")
        var_ready = sem("var_ready")
        veps_ready = sem("veps_ready")
        rstd_ready = sem("rstd_ready")
        x1_ready = sem("x1_ready")
        x1_stored = [sem(f"x1_stored{h}") for h in range(2)]
        eps_added = sem("eps_added")
        block = ctx.enter_context(nc.Block())

        def over_batches(eng, body):
            with eng.Fori(0, last_batch) as b:
                body(b, False)
            body(last_batch, True)


        def slot_of(v):
            return (v + (v >= SHIFTS[0]) + (v >= SHIFTS[1])) % RING

        def units_before(v):
            return max(w for w in range(v - UNITS, v) if slot_of(w % UNITS) == slot_of(v)) + 1

        def at_unit(layer, j, u):
            return at[:, UT * u:UT * u + UT, j * CH:(j + 1) * CH]

        def ring_view(ring, layer, j, u):
            return ring[:, slot_of(layer * LU + j * UPC + u), :].rearrange("p (t n) -> p t n", t=UT)

        def pool_splits(layer, j, u):
            return layer == 1 and u in POOL_UNITS[j]

        def pool_units(n):
            return sum(pool_splits(v // LU, v % LU // UPC, v % UPC) for v in range(n))

        POOL_TOTAL = pool_units(UNITS)

        def wait_lo(eng, b, n):
            p = pool_units(n)
            if n - p:
                eng.wait_ge(dve_lo, b * (UNITS - POOL_TOTAL) + n - p)
            if p:
                eng.wait_ge(pool_lo, b * POOL_TOTAL + p)


        def place_of(k, first):
            return FIRST_PLACES[k] if first else LATER_PLACES[k]

        def before_in_place(k, first):
            return max((n for n in range(k) if place_of(n, first) == place_of(k, first)), default=None)

        def rows_here(b, k, first):
            s = place_of(k, first)
            loads = (FIRST_PLACES if first else LATER_PLACES)[:k + 1].count(s)
            if not first:
                loads += FIRST_PLACES.count(s) + b * LATER_PLACES.count(s)
            return rows_in[s], loads * 16 * QUADS

        def last_rows_here(b, k):
            s = place_of(k, False)
            assert s == place_of(k, True) and k == max(n for n in range(NT) if LATER_PLACES[n] == s)
            return rows_in[s], (FIRST_PLACES.count(s) + b * LATER_PLACES.count(s)) * 16 * QUADS

        def x_here(b, t, residual):
            slot = t % (XS if residual else XF)
            per_batch = NT // XF + (NT // XS if slot < XS else 0)
            return x_loaded[slot], (b * per_batch + (NT // XF + t // XS if residual else t // XF) + 1) * 16

        def rows_view(k, first):
            return places[place_of(k, first)]

        ACT_TILES = NT - len(DVE_SUMS)

        def sums(b, k):
            d = sum(n <= k for n in DVE_SUMS)
            if k in DVE_SUMS:
                return dve_summed, b * len(DVE_SUMS) + d
            return act_summed, b * ACT_TILES + k + 1 - d


        def steps():
            for layer in range(2):
                for j in range(NJ):
                    for u in range(UPC):
                        if layer or j or u >= AHEAD:
                            yield layer, j, u

        def feats_at(layer, j, u):
            if layer == 0 and j == 0:
                return [(0, t) for t in range(UT * u, UT * u + UT)]
            if layer == 0 and j == NJ - 1 and u >= RING + 1:
                p = u - RING - 1
                return [(1, t) for t in range(UT * p, UT * p + UT)]
            if layer == 1 and j == 0:
                pairs = PAIRS_AT.get(u, [])
                return [(1, t) for p in pairs for t in range(UT * p, UT * p + UT)]
            return []

        def scaled_at(layer, j, u):
            c = layer * NJ + j
            if c == NJ:
                now = {4: [0, 1], 5: [2, 3]}.get(u, [])
                late = [TPC * (c - 2) + 3] if u == 0 else []
                return late + [TPC * (c - 1) + i for i in now]
            if layer:
                return []
            out = []
            if c >= 2 and u == 0:
                out.append(TPC * (c - 2) + 3)
            if c >= 1 and u >= 5:
                out.append(TPC * (c - 1) + u - 5)
            return out

        def normalised_at(layer, j, u):
            c = layer * NJ + j
            if 2 <= c <= NJ and u == 1:
                return [c - 2]
            if c == NJ and u == 6:
                return [NJ - 1]
            return []

        @block.sync
        def _(sp):
            sp.dma_start(w0_in, g["w0"].rearrange("(k p) d -> p k d", p=P)).then_inc(consts_in, 16)
            sp.dma_start(bias[:, :], g["bias0"].to_broadcast([P, D])).then_inc(consts_in, 16)
            sp.dma_start(eps_sb[:, :], g["eps"].to_broadcast([P, 1])).then_inc(consts_in, 16)
            with nc.allow_non_contiguous_dma(reason="a hidden unit's bias and weight go to its partition"):
                sp.dma_start(b1_sb[:, :], g["b1"].rearrange("(h p) -> p h", p=P)).then_inc(consts_in, 16)
                sp.dma_start(rms_sb[:, :], g["rms_w"].rearrange("(h p) -> p h", p=P)).then_inc(consts_in, 16)

            def wait_all(*waits):
                values = [v if isinstance(v, int) else sp.to_reg(v) for _, v in waits]
                for (semaphore, _), value in zip(waits, values):
                    sp.wait_ge(semaphore, value)

            def load_rows(b, k, first, *waits):
                rows = [adj_rows[b, k, q] for q in range(QUADS)]
                wait_all(*waits)
                for q in range(QUADS):
                    sp.dma_start(rows_view(k, first)[:, q, :], rows[q]).then_inc(rows_in[place_of(k, first)], 16)

            def rows_used(b, k):
                return sums(b, k), (transposed, b * NT + T_ORDER.index(k) + 1)

            def load_x(b, t, residual, *waits):
                if residual and t < XS:
                    free = feat_lo, b * 2 * NT + NT - XF + t + 1
                elif residual:
                    free = summed, b * NT + t - XS + 2
                elif t < XF:
                    free = summed, b * NT + 1
                else:
                    free = feat_lo, b * 2 * NT + t - XF + 1
                src = x_rows[b, t]
                wait_all(*waits, free)
                slot = t % (XS if residual else XF)
                sp.dma_start(x_in[:, slot, :], src).then_inc(x_loaded[slot], 16)

            def store_x1(b, j):
                dst = x1_scratch[b * NJ + j]
                src = x1[:, TPC * j:TPC * (j + 1), :].rearrange("p t d -> p (t d)")
                sp.wait_ge(x1_ready, b * NT + TPC * (j + 1))
                sp.dma_start(dst, src).then_inc(x1_stored[j // 2], 16)

            def half_stored(b, h):
                return (x1_stored[h], (b + 1) * (NJ // 2) * 16), (feat_lo, b * 2 * NT + NT + (h + 1) * (NT // 2))

            for k in range(NT):
                before = before_in_place(k, True)
                load_rows(0, k, True, *([] if before is None else rows_used(0, before)))
            for t in range(XF):
                load_x(0, t, False, (w0_ready, 1))

            def body(b, is_last):
                if not is_last:
                    sp.to_reg(b * (N * D) * 4)
                for t in range(XF, NT):
                    load_x(b, t, False)
                for j in range(NJ):
                    for t in range(TPC * j, TPC * (j + 1)):
                        load_x(b, t, True)
                    if j:
                        store_x1(b, j - 1)
                if is_last:
                    store_x1(b, NJ - 1)
                    load_for_dense()
                    return
                load_rows(b + 1, 0, False, *half_stored(b, 0))
                store_x1(b, NJ - 1)
                load_rows(b + 1, 1, False, (summed, (b + 1) * NT + 1))
                load_rows(b + 1, 2, False, *half_stored(b, 1))
                for k in range(3, NT - 2):
                    load_rows(b + 1, k, False, *rows_used(b + 1, before_in_place(k, False)))
                    if k == LOAD_X:
                        last_third = max(n for n in range(NT) if LATER_PLACES[n] == THIRD_PLACE)
                        for t in range(XS):
                            load_x(b + 1, t, False, *rows_used(b + 1, last_third))
                load_rows(b + 1, NT - 2, False, (unit_free, (b + 1) * UNITS - UPC + 4 // UT + RING))
                load_rows(b + 1, NT - 1, False, (agg_stored, (b * NJ + NJ) * 16))
                for t in range(XS, XF):
                    load_x(b + 1, t, False)

            def load_for_dense():
                sp.wait_ge(x1_stored[0], B * (NJ // 2) * 16)
                sp.wait_ge(x1_stored[1], B * (NJ // 2) * 16)
                sp.wait_ge(feat_lo, B * 2 * NT)
                sp.dma_start(w1_in, g["w1"].rearrange("(k p) h -> p k h", p=P)).then_inc(w_in, 16)
                sp.dma_start(w2_in, g["w2"].rearrange("(h p) d -> p h d", p=P)).then_inc(w_in, 16)
                wait_lo(sp, last_batch, LU + (NJ - 1) * UPC + 3)
                sp.wait_ge(agg_stored, 3 * 16)
                for i in range(2):
                    sp.dma_start(agg_in[:, i, :, :, :].bitcast(F32).rearrange("p h k n -> p (h k n)"), agg_scratch[i])\
                        .then_inc(agg_here[i], 16)

            over_batches(sp, body)
            for stored in x1_stored:
                sp.wait_ge(stored, B * NJ // 2 * 16)

        @block.scalar
        def _(act):
            def sum_rows(b, k, first):
                if k in DVE_SUMS:
                    return
                act.wait_ge(*rows_here(b, k, first))
                _, count = sums(b if first else b + 1, k)
                if not (first and k == 0):
                    act.wait_ge(act_summed, count - 1)
                if k == 0 and not first:
                    act.wait_ge(y_used, (b + 1) * NT + 2)
                for q in range(QUADS):
                    last = act.activation(y_ps[q][:, :], rows_view(k, first)[:, q, :], ACT.Copy,
                                          accum_out=part[:, k, q:q + 1])
                last.then_inc(act_summed, 1)

            def split_feat(b, layer, t):
                if layer == 1 or t < AHEAD * UT and not (isinstance(b, int) and b == 0):
                    act.wait_ge(unit_free, b * UNITS + layer * LU - UPC + t // UT + 1 + RING)
                if layer == 0:
                    if t in (0, UT):
                        act.wait_ge(dinv_ready, 2 * b + (1 if t == 0 else 2))
                    if t == 0:
                        act.wait_ge(transposed, b * NT + T_ORDER.index(NT - 2) + 1)
                    act.wait_ge(*x_here(b, t, False))
                    act.activation(feat[:, t, 0, :], x_in[:, t % XF, :], ACT.Copy,
                                   scale=dinv[:, t:t + 1]).then_inc(feat_hi, 1)
                else:
                    act.wait_ge(x1_ready, b * NT + t + 1)
                    act.copy(feat[:, t, 0, :], x1[:, t, :]).then_inc(feat_hi, 1)

            def split_unit(b, layer, j, u):
                if layer == 0 and u == 0:
                    act.wait_ge(transposed, b * NT + (TPC * (j + 1) if j < NJ - 1 else NT))
                if layer == 1 and u == 0:
                    act.wait_ge(eps_added, b * NT + TPC * (j + 1))
                act.wait_ge(unit_free, b * UNITS + RING + units_before(layer * LU + j * UPC + u))
                act.copy(ring_view(unit_hi, layer, j, u), at_unit(layer, j, u)).then_inc(hi_ready, 1)

            def split_agg(b, c):
                act.wait_ge(unit_free, b * UNITS + UPC * (c + 1) + RING)
                if 1 <= c <= NJ:
                    act.wait_ge(y_ready, b * NT + TPC * c)
                elif c:
                    act.wait_ge(agg_stored, (b * NJ + (c - NJ) + 1) * 16)
                if c == CPB - 1 or c == 0:
                    nb = b + 1 if c else b
                    if c == 0 or not (isinstance(b, int) and b == last_batch):
                        act.wait_ge(transposed, nb * NT + T_ORDER.index(NT - 1) + 1)
                        act.wait_ge(*sums(nb, NT - 1))
                if c == 0:
                    act.wait_ge(agg_stored, (b * NJ + 1) * 16)
                for ob in range(DK):
                    last = act.copy(agg[:, 0, ob, :], agg_ps[c % 2][ob][:, :])
                last.then_inc(agg_hi, 1)

            def store_agg(b, c):
                act.wait_ge(agg_lo, b * CPB + c + 3)
                act.dma_start(agg_scratch[b * NJ + (c - NJ)],
                              agg[:, :, :, :].bitcast(F32).rearrange("p h k n -> p (h k n)")).then_inc(agg_stored, 16)

            def scale_y(b, t):
                act.wait_ge(y_ready, b * NT + t + 1)
                act.wait_ge(y_used, b * NT + t + 1)
                act.activation(y_lo[:, t % 2, :], y_ps[t % TPC][:, D:2 * D], ACT.Copy,
                               scale=dinv[:, t:t + 1]).then_inc(ylo_ready, 1)

            def ahead(b, before):
                split_unit(b, 0, 0, 0)
                for t in range(UT):
                    split_feat(b, 0, t)
                split_unit(b, 0, 0, 1)
                if before is not None:
                    split_agg(before, CPB - 1)
                for t in range(UT, UT * AHEAD):
                    split_feat(b, 0, t)

            act.sem_inc(agg_stored, 16)
            act.wait_ge(consts_in, 5 * 16)
            act.copy(w0s[:, :, 0, :], w0_in).then_inc(w0_hi, 1)
            for k in range(NT):
                sum_rows(0, k, True)
            ahead(0, None)

            def body(b, is_last):
                split_unit(b, 0, 0, AHEAD - 1)
                for layer, j, u in steps():
                    c = layer * NJ + j
                    if c and u == 2:
                        split_agg(b, c - 1)
                    if c > NJ and u == 3:
                        store_agg(b, c - 1)
                    for t in scaled_at(layer, j, u):
                        scale_y(b, t)
                    for ly, t in feats_at(layer, j, u):
                        split_feat(b, ly, t)
                    split_unit(b, layer, j, u)
                    if layer and not is_last:
                        for k in SUM_AT.get((j, u), []):
                            sum_rows(b, k, False)
                    if is_last and c == CPB - 1 and u == 2:
                        act.wait_ge(w_in, 2 * 16)
                        wait_lo(act, b, LU + (NJ - 1) * UPC + 2)
                        act.copy(w1s[:, 0, :, :], w1_in).then_inc(w_hi, 1)
                        act.copy(w2s[:, :, 0, :], w2_in).then_inc(w_hi, 1)
                if not is_last:
                    ahead(b + 1, b)
                else:
                    split_agg(b, CPB - 1)
                store_agg(b, CPB - 1)

            over_batches(act, body)

        @block.gpsimd
        def _(pool):
            pool.memset(minus_half[:, :], -0.5)
            pool.memset(ln_eps[:, :], LN_EPS)
            pool.memset(fold[:, :], 0.0).then_inc(pool_consts, 1)
            pool.memset(ident[:, :], 0.0).then_inc(pool_consts, 1)
            pool.wait_ge(pool_consts, 2)
            pool.affine_select(out=ident[:, :], in_=ident[:, :], compare_op=ALU.not_equal, fill=1.0, base=0,
                               pattern=[[-1, P]], channel_multiplier=1).then_inc(pool_consts, 1)
            for n, s in enumerate(range(-(QUADS - 1), QUADS)):
                if n:
                    pool.wait_ge(pool_consts, 3 + n)
                pool.affine_select(out=fold[:, :], in_=fold[:, :], compare_op=ALU.not_equal, fill=1.0,
                                   base=-QP * s, pattern=[[-1, P]], channel_multiplier=1).then_inc(pool_consts, 1)
            pool.wait_ge(consts_in, 5 * 16)

            def invert(b):
                pool.wait_ge(deg_ready, b + 1)
                for cols in (slice(0, UT), slice(UT, NT)):
                    pool.tensor_tensor(dinv[:, cols], deg[:, cols], minus_half[:, cols], ALU.pow)\
                        .then_inc(dinv_ready, 1)

            invert(0)

            def body(b, is_last):
                for j in range(NJ):
                    for i in range(TPC):
                        t = TPC * j + i
                        pool.wait_ge(*x_here(b, t, True))
                        pool.tensor_tensor(x_in[:, t % XS, :], x_in[:, t % XS, :], bias[:, :], ALU.add)\
                            .then_inc(biased, 1)
                    pool.wait_ge(var_ready, b * NJ + j + 1)
                    pool.tensor_tensor(var_eps[:, :], mean_var[:, :, 1], ln_eps[:, :], ALU.add).then_inc(veps_ready, 1)
                    pool.wait_ge(veps_ready, b * NJ + j + 1)
                    pool.tensor_tensor(rstd[:, :], var_eps[:, :], minus_half[:, 0:TPC], ALU.pow)\
                        .then_inc(rstd_ready, 1)
                for j in range(NJ):
                    for u in POOL_UNITS[j]:
                        pool.wait_ge(hi_ready, b * UNITS + LU + j * UPC + u + 1)
                        pool.tensor_tensor(ring_view(unit_lo, 1, j, u), at_unit(1, j, u),
                                           ring_view(unit_hi, 1, j, u).bitcast(F32),
                                           ALU.subtract).then_inc(pool_lo, 1)
                if not is_last:
                    invert(b + 1)

            over_batches(pool, body)

        @block.vector
        def _(dve):
            dve.sem_inc(summed, 1)
            dve.sem_inc(y_used, 2)
            dve.sem_inc(agg_lo, 2)

            def transpose_rows(b, k, first, late=False):
                dve.wait_ge(*(last_rows_here(b, k) if late else rows_here(b, k, first)))
                src = rows_view(k, first).rearrange("p q (t c) -> p q t c", c=QP)
                dst = at[:, :, k * P:(k + 1) * P].rearrange("p t (q a) -> p q t a", a=QP)
                dve.transpose(dst, src).then_inc(transposed, 1)

            def sum_rows(b, k, first):
                if k not in DVE_SUMS:
                    return
                dve.wait_ge(*rows_here(b, k, first))
                dve.tensor_reduce(part[:, k, :], rows_view(k, first), axis=mybir.AxisListType.X, op=ALU.add)\
                    .then_inc(dve_summed, 1)

            def split_feat(b, layer, t):
                dve.wait_ge(feat_hi, b * 2 * NT + layer * NT + t + 1)
                hi = feat[:, t, 0, :].bitcast(F32)
                if layer == 0:
                    last = dve.scalar_tensor_tensor(feat[:, t, 1, :], x_in[:, t % XF, :], dinv[:, t:t + 1], hi,
                                                    op0=ALU.mult, op1=ALU.subtract)
                    last.then_inc(feat_lo, 1)
                else:
                    dve.tensor_tensor(feat[:, t, 1, :], x1[:, t, :], hi, ALU.subtract).then_inc(feat_lo, 1)

            def split_unit(b, layer, j, u):
                if pool_splits(layer, j, u):
                    return
                dve.wait_ge(hi_ready, b * UNITS + layer * LU + j * UPC + u + 1)
                dve.tensor_tensor(ring_view(unit_lo, layer, j, u), at_unit(layer, j, u),
                                  ring_view(unit_hi, layer, j, u).bitcast(F32),
                                  ALU.subtract).then_inc(dve_lo, 1)

            def find_deg(b):
                dve.wait_ge(sums_folded, b + 1)
                folded = fold_ps[:, 0:NT * QUADS].rearrange("p (t q) -> p t q", q=QUADS)
                for q in range(QUADS):
                    rows = slice(q * QP, (q + 1) * QP)
                    last = dve.tensor_scalar(deg[rows, :], folded[rows, :, q], DEG_EPS, None, op0=ALU.add)
                last.then_inc(deg_ready, 1)

            def split_agg(b, c):
                dve.wait_ge(agg_hi, b * CPB + c + 1)
                for ob in range(DK):
                    last = dve.tensor_tensor(agg[:, 1, ob, :], agg_ps[c % 2][ob][:, :],
                                             agg[:, 0, ob, :].bitcast(F32), ALU.subtract)
                last.then_inc(agg_lo, 1)

            def ahead(b, before):
                split_unit(b, 0, 0, 0)
                for t in range(UT):
                    split_feat(b, 0, t)
                split_unit(b, 0, 0, 1)
                if before is not None:
                    split_agg(before, CPB - 1)
                for t in range(UT, UT * AHEAD):
                    split_feat(b, 0, t)

            dve.wait_ge(w0_hi, 1)
            dve.tensor_tensor(w0s[:, :, 1, :], w0_in, w0s[:, :, 0, :].bitcast(F32), ALU.subtract)\
                .then_inc(w0_ready, 1)
            for k in range(NT - TPC):
                sum_rows(0, k, True)
                transpose_rows(0, k, True)
            for k in range(NT - TPC, NT):
                sum_rows(0, k, True)
            for k in (NT - 2, NT - 1):
                transpose_rows(0, k, True)
            find_deg(0)
            ahead(0, None)

            def body(b, is_last):
                def add_up(t):
                    dve.wait_ge(ylo_ready, b * NT + t + 1)
                    dve.scalar_tensor_tensor(x1[:, t, :], y_ps[t % TPC][:, 0:D], dinv[:, t:t + 1], y_lo[:, t % 2, :],
                                             op0=ALU.mult, op1=ALU.add).then_inc(y_used, 1)
                    dve.wait_ge(biased, b * NT + t + 1)
                    dve.wait_ge(y_used, b * NT + t + 3)
                    last = dve.tensor_tensor(x1[:, t, :], x1[:, t, :], x_in[:, t % XS, :], ALU.add)
                    last.then_inc(summed, 1)
                    dve.wait_ge(summed, b * NT + t + 2)
                    dve.bn_stats(stats[:, :], x1[:, t, :]).then_inc(stats_done, 1)
                    dve.wait_ge(stats_done, b * NT + t + 1)
                    dve.memset(wait_here[:, :], 0.0)
                    last = dve.bn_aggr(mean_var[:, t % TPC, :], stats[:, :])
                    if t % TPC == TPC - 1:
                        last.then_inc(var_ready, 1)

                def normalise(j):
                    dve.wait_ge(rstd_ready, b * NJ + j + 1)
                    for i in range(TPC):
                        t = TPC * j + i
                        dve.tensor_scalar(x1[:, t, :], x1[:, t, :], mean_var[:, i, 0:1], rstd[:, i:i + 1],
                                          op0=ALU.subtract, op1=ALU.mult).then_inc(x1_ready, 1)

                def add_eps(j):
                    for t in range(TPC * j, TPC * (j + 1)):
                        diag = at[:, t, t * P:(t + 1) * P]
                        dve.scalar_tensor_tensor(diag, ident[:, :], eps_sb[:, 0:1], diag, op0=ALU.mult,
                                                 op1=ALU.add).then_inc(eps_added, 1)

                def columns_free(j):
                    wait_lo(dve, b, LU + UPC * (j + 1))

                split_unit(b, 0, 0, AHEAD - 1)
                for layer, j, u in steps():
                    c = layer * NJ + j
                    if (layer == 0 and j or c == NJ) and u == 3:
                        add_eps(j - 1 if layer == 0 else NJ - 1)
                    if c and u == 2:
                        split_agg(b, c - 1)
                    for t in scaled_at(layer, j, u):
                        add_up(t)
                    for i in normalised_at(layer, j, u):
                        normalise(i)
                    for ly, t in feats_at(layer, j, u):
                        split_feat(b, ly, t)
                    split_unit(b, layer, j, u)
                    if layer == 0:
                        for k in LATE_T_AT.get((j, u), []):
                            transpose_rows(b, k, False, late=True)
                    if is_last and c == CPB - 1 and u == 4:
                        dve.wait_ge(w_hi, 1)
                        dve.tensor_tensor(w1s[:, 1, :, :], w1_in, w1s[:, 0, :, :].bitcast(F32), ALU.subtract)\
                            .then_inc(w_ready, 1)
                        dve.wait_ge(w_hi, 2)
                        dve.tensor_tensor(w2s[:, :, 1, :], w2_in, w2s[:, :, 0, :].bitcast(F32), ALU.subtract)\
                            .then_inc(w_ready, 1)
                    if layer and not is_last:
                        for k in SUM_AT.get((j, u), []):
                            sum_rows(b, k, False)
                        for k in T_AT.get((j, u), []):
                            if k % TPC == 0:
                                columns_free(k // TPC)
                            transpose_rows(b, k, False)
                if not is_last:
                    columns_free(NJ - 1)
                    transpose_rows(b, NT - 2, False)
                    transpose_rows(b, NT - 1, False)
                    find_deg(b + 1)
                    ahead(b + 1, b)
                else:
                    split_agg(b, CPB - 1)

            over_batches(dve, body)

        @block.tensor
        def _(pe):
            pe.sem_inc(unit_free, RING)
            pe.wait_ge(w0_ready, 1)
            pe.wait_ge(pool_consts, 3 + 2 * QUADS - 1)

            def fold_sums(b):
                pe.wait_ge(act_summed, (b + 1) * ACT_TILES)
                pe.wait_ge(dve_summed, (b + 1) * len(DVE_SUMS))
                pe.wait_ge(y_used, b * NT + 2)
                pe.matmul(fold_ps[:, 0:NT * QUADS], fold[:, :], part[:, :, :].rearrange("p t q -> p (t q)"),
                          start=True, stop=True).then_inc(sums_folded, 1)

            fold_sums(0)

            def body(b, is_last):
                def times_w(j):
                    pe.wait_ge(agg_lo, b * CPB + j + 3)
                    if j == 0:
                        pe.wait_ge(deg_ready, b + 1)
                    pe.wait_ge(y_used, b * NT + TPC * j + 2)
                    for i in range(TPC):
                        cols = slice(i * P, (i + 1) * P)
                        for k in range(DK):
                            pe.matmul(y_ps[i][:, :], agg[:, 0, k, cols], w0s[:, k, :, :].rearrange("p h d -> p (h d)"),
                                      start=(k == 0), stop=False)
                            last = pe.matmul(y_ps[i][:, 0:D], agg[:, 1, k, cols], w0s[:, k, 0, :],
                                             start=False, stop=(k == DK - 1))
                        last.then_inc(y_ready, 1)

                for layer in range(2):
                    for j in range(NJ):
                        c = layer * NJ + j
                        for u in range(UPC):
                            if u == (1 if c == NJ else 2) and 1 <= c <= NJ:
                                times_w(c - 1)
                            if u == 0:
                                pe.wait_ge(agg_lo, b * CPB + c + 1)
                            n = layer * LU + j * UPC + u + 1
                            if pool_splits(layer, j, u):
                                pe.wait_ge(pool_lo, b * POOL_TOTAL + pool_units(n))
                            else:
                                pe.wait_ge(dve_lo, b * (UNITS - POOL_TOTAL) + n - pool_units(n))
                            if j == 0:
                                pe.wait_ge(feat_lo, b * 2 * NT + layer * NT + UT * (u + 1))
                            hi, lo = ring_view(unit_hi, layer, j, u), ring_view(unit_lo, layer, j, u)
                            for tt in range(UT):
                                t = UT * u + tt
                                for ob in range(DK):
                                    out = agg_ps[c % 2][ob][:, :]
                                    f_hi = feat[:, t, 0, ob * P:(ob + 1) * P]
                                    f_lo = feat[:, t, 1, ob * P:(ob + 1) * P]
                                    pe.matmul(out, f_hi, hi[:, tt, :], start=(t == 0), stop=False)
                                    pe.matmul(out, f_hi, lo[:, tt, :], start=False, stop=False)
                                    last = pe.matmul(out, f_lo, hi[:, tt, :], start=False, stop=(t == NT - 1))
                            last.then_inc(unit_free, 1)
                if not is_last:
                    fold_sums(b + 1)

            over_batches(pe, body)


def dense(nc, g):
    B, D, H, CH, NJ, TPC, DK, HK = (g[k] for k in ("B", "D", "H", "CH", "NJ", "TPC", "DK", "HK"))
    agg_scratch, x1_scratch, y_rows = g["agg_scratch"], g["x1_scratch"], g["y_rows"]
    ident, psum, in_at, w1s, w2s, agg_in, b1_sb, rms_sb, agg_stored, agg_here, w_ready = (
        g[k] for k in ("ident", "psum", "in_at", "w1s", "w2s", "agg_in", "b1_sb", "rms_sb", "agg_stored", "agg_here",
                       "w_ready"))
    NC = B * NJ

    with ExitStack() as ctx:
        def sb(name, shape, dt=F32):
            return ctx.enter_context(nc.sbuf_tensor(name, shape, dt))

        def sem(name):
            return ctx.enter_context(nc.semaphore(name))

        b2_sb = sb("b2_sb", [P, D])
        ones = sb("ones", [P, P])
        ones_r = sb("ones_r", [P, P], F32R)
        minus_half4 = sb("minus_half4", [P, TPC])
        wait_here2 = sb("wait_here2", [P, 1])
        ln_eps4 = sb("ln_eps4", [P, TPC])
        x1_in = sb("x1_in", [P, 2, TPC, D])
        hid = in_at("hid", [P, 2, HK, CH], 10)
        s_hi = in_at("s_hi", [P, HK, CH], 6, F32R)
        s_lo = in_at("s_lo", [P, HK, CH], 8, F32R)
        sq = in_at("sq", [P, HK, CH], 14)
        sum_sq = sb("sum_sq", [P, 2, CH])
        mean_sq = sb("mean_sq", [P, TPC])
        rms_inv = sb("rms_inv", [P, TPC])
        diag = sb("diag", [P, 2, CH], F32R)
        out = sb("out", [P, 2, TPC, D])
        bstats = sb("bstats", [P, TPC, 6])
        mv = sb("mv", [P, TPC, 2])
        vare = sb("vare", [P, TPC])
        rstd2 = sb("rstd2", [P, TPC])

        h_ps = psum[0:2]
        o_ps = psum[2:6]
        sq_ps = psum[6]
        r_ps = psum[7]
        last_ps = [*h_ps, sq_ps, r_ps]

        b2_in = sem("b2_in")
        ones_set = sem("ones_set")
        x1_here = [sem(f"x1_here{s}") for s in range(2)]
        h_done = sem("h_done")
        h_ready = sem("h_ready")
        squared = sem("squared")
        sq_added = sem("sq_added")
        sq_summed = sem("sq_summed")
        mean_ready = sem("mean_ready")
        rms_ready = sem("rms_ready")
        ones_r_set = sem("ones_r_set")
        diag_hi = sem("diag_hi")
        diag_ready = sem("diag_ready")
        r_spread = sem("r_spread")
        z_ready = sem("z_ready")
        act_ready = sem("act_ready")
        shi_ready = sem("shi_ready")
        slo_ready = sem("slo_ready")
        w2_done = sem("w2_done")
        x1_biased = sem("x1_biased")
        half_added = sem("half_added")
        o_read = sem("o_read")
        o_stats = sem("o_stats")
        o_var = sem("o_var")
        vare_ready = sem("vare_ready")
        rstd2_ready = sem("rstd2_ready")
        out_ready = sem("out_ready")
        out_stored = [sem(f"out_stored{s}") for s in range(2)]
        block = ctx.enter_context(nc.Block())

        def wait(eng, semaphore, value):
            if not isinstance(value, int) or value > 0:
                eng.wait_ge(semaphore, value)

        def over_steps(eng, step):
            for o in range(NJ):
                step(0, o)
            if B > 2:
                with eng.Fori(1, B) as m:
                    for o in range(NJ):
                        step(m, o)
            elif B == 2:
                for o in range(NJ):
                    step(1, o)
            for o in range(3):
                step(B, o)

        def product_banks(m, o):
            return last_ps if isinstance(m, int) and NJ * m + o == NC - 1 else o_ps

        def there(m, o, back):
            if isinstance(m, int):
                return 0 <= NJ * m + o - back < NC
            return True

        def used(m, o):
            return m * (NJ // 2) + o // 2

        @block.sync
        def _(sp):
            sp.dma_start(b2_sb[:, :], g["b2"].to_broadcast([P, D])).then_inc(b2_in, 16)

            def load_agg(m, o):
                src = agg_scratch[NJ * m + o]
                waits = (agg_stored, (NJ * m + o + 2) * 16), (h_done, (NJ * m + o - 1) * HK)
                values = [v if isinstance(v, int) else sp.to_reg(v) for _, v in waits]
                for (semaphore, _), value in zip(waits, values):
                    wait(sp, semaphore, value)
                sp.dma_start(agg_in[:, o % 2, :, :, :].bitcast(F32).rearrange("p h k n -> p (h k n)"),
                             src).then_inc(agg_here[o % 2], 16)

            def step(m, o):
                if there(m, o, 0) and not (isinstance(m, int) and m == 0 and o < 2):
                    load_agg(m, o)
                if there(m, o, 2):
                    wait(sp, half_added, (NJ * m + o - 3) * TPC)
                    sp.dma_start(x1_in[:, o % 2, :, :].rearrange("p t d -> p (t d)"),
                                 x1_scratch[NJ * m + o - 2]).then_inc(x1_here[o % 2], 16)
                if there(m, o, 3):
                    b, j = (m, o - 3) if o >= 3 else (m - 1, o - 3 + NJ)
                    for t in range(TPC):
                        wait(sp, out_ready, (NJ * m + o - 3) * TPC + t + 1)
                        sp.dma_start(y_rows[b, TPC * j + t], out[:, (o - 3) % 2, t, :])\
                            .then_inc(out_stored[(o - 3) % 2], 16)

            over_steps(sp, step)
            for s in range(2):
                sp.wait_ge(out_stored[s], NC // 2 * TPC * 16)

        @block.scalar
        def _(act):
            def activate(m, o, h):
                n = (NJ * m + o) * HK + h
                cur = hid[:, o % 2, h, :]
                act.wait_ge(z_ready, n + 1)
                act.activation(cur, cur, ACT.Silu, scale=rms_sb[:, h:h + 1]).then_inc(act_ready, 1)
                act.wait_ge(act_ready, n + 1)
                wait(act, w2_done, n - HK + 1)
                act.copy(s_hi[:, h, :], cur).then_inc(shi_ready, 1)

            def square(m, o, h):
                i = NJ * m + o
                if isinstance(m, int) and i < FILL:
                    return
                act.wait_ge(h_ready, i * HK + h + 1)
                if h == 0:
                    wait(act, sq_summed, i - 1)
                    if isinstance(m, int) and i == FILL:
                        act.wait_ge(squared, FILL * HK)
                else:
                    wait(act, sq_added, (i - 1) * (HK - 1) + h)
                dst = sq[:, h, :] if h else sum_sq[:, o % 2, :]
                act.activation(dst, hid[:, o % 2, h, :], ACT.Square).then_inc(squared, 1)

            def step(m, o):
                i = NJ * m + o
                if there(m, o, 0):
                    for h in range(HK):
                        act.wait_ge(h_done, i * HK + h + 1)
                        wait(act, slo_ready, (i - 2) * HK + h + 1)
                        act.activation(hid[:, o % 2, h, :], h_ps[h % 2][:, :], ACT.Identity,
                                       bias=b1_sb[:, h:h + 1]).then_inc(h_ready, 1)
                        if h:
                            square(m, o, h - 1)
                    square(m, o, HK - 1)
                if there(m, o, 1):
                    for h in range(HK):
                        activate(m, o - 1, h)

            over_steps(act, step)

        @block.gpsimd
        def _(pool):
            pool.memset(ones[:, :], 1.0).then_inc(ones_set, 1)
            pool.memset(minus_half4[:, :], -0.5).then_inc(ones_set, 1)
            pool.memset(ln_eps4[:, :], LN_EPS).then_inc(ones_set, 1)
            pool.wait_ge(ones_set, 3)
            pool.wait_ge(b2_in, 16)

            def add_square(m, o, h):
                i = NJ * m + o
                pool.wait_ge(squared, i * HK + h + 1)
                wait(pool, sq_added, i * (HK - 1) + h - 1)
                pool.tensor_tensor(sum_sq[:, o % 2, :], sum_sq[:, o % 2, :], sq[:, h, :], ALU.add)\
                    .then_inc(sq_added, 1)

            def step(m, o):
                i = NJ * m + o
                if there(m, o, 1):
                    pool.wait_ge(mean_ready, i)
                    pool.tensor_tensor(rms_inv[:, :], mean_sq[:, :], minus_half4[:, :], ALU.pow).then_inc(rms_ready, 1)
                if there(m, o, 0):
                    for h in (1, 2):
                        add_square(m, o, h)
                if there(m, o, 3):
                    pool.wait_ge(o_var, i - 2)
                    pool.tensor_tensor(vare[:, :], mv[:, :, 1], ln_eps4[:, :], ALU.add).then_inc(vare_ready, 1)
                    pool.wait_ge(vare_ready, i - 2)
                    pool.tensor_tensor(rstd2[:, :], vare[:, :], minus_half4[:, :], ALU.pow).then_inc(rstd2_ready, 1)
                if there(m, o, 0):
                    for h in range(3, HK):
                        add_square(m, o, h)
                if there(m, o, 2):
                    p = o % 2
                    pool.wait_ge(x1_here[p], (used(m, o - 2) + 1) * 16)
                    for t in range(TPC):
                        pool.tensor_tensor(x1_in[:, p, t, :], x1_in[:, p, t, :], b2_sb[:, :], ALU.add)\
                            .then_inc(x1_biased, 1)

            over_steps(pool, step)

        @block.vector
        def _(dve):
            def scale(m, o, h):
                cur = hid[:, o % 2, h, :]
                if h == 0:
                    dve.wait_ge(r_spread, NJ * m + o + 1)
                dve.tensor_tensor(cur, cur, r_ps[:, :], ALU.mult).then_inc(z_ready, 1)

            def square(m, o, blocks):
                i = NJ * m + o
                if isinstance(m, int) and i < FILL:
                    for h in blocks:
                        dve.wait_ge(h_ready, i * HK + h + 1)
                        cur = hid[:, o % 2, h, :]
                        dst = sq[:, h, :] if h else sum_sq[:, o % 2, :]
                        if h:
                            wait(dve, sq_added, (i - 1) * (HK - 1) + h)
                        dve.tensor_tensor(dst, cur, cur, ALU.mult).then_inc(squared, 1)

            def split(m, o, h):
                dve.wait_ge(shi_ready, (NJ * m + o) * HK + h + 1)
                dve.tensor_tensor(s_lo[:, h, :], hid[:, o % 2, h, :], s_hi[:, h, :].bitcast(F32), ALU.subtract)\
                    .then_inc(slo_ready, 1)

            def add_up(m, o, t):
                n = (NJ * m + o) * TPC + t
                v = out[:, o % 2, t, :]
                bank = product_banks(m, o)[t]
                if t == 0:
                    dve.wait_ge(w2_done, (NJ * m + o + 1) * HK)
                    wait(dve, out_stored[o % 2], used(m, o) * TPC * 16)
                dve.wait_ge(x1_biased, n + 1)
                dve.tensor_tensor(v, bank[:, 0:D], x1_in[:, o % 2, t, :], ALU.add).then_inc(half_added, 1)
                dve.wait_ge(half_added, n + 1)
                dve.tensor_tensor(v, v, bank[:, D:2 * D], ALU.add).then_inc(o_read, 1)
                dve.wait_ge(o_read, n + 1)
                dve.bn_stats(bstats[:, t, :], v).then_inc(o_stats, 1)
                dve.wait_ge(o_stats, n + 1)
                dve.memset(wait_here2[:, :], 0.0)
                last = dve.bn_aggr(mv[:, t, :], bstats[:, t, :])
                if t == TPC - 1:
                    last.then_inc(o_var, 1)

            dve.wait_ge(ones_set, 3)
            dve.tensor_copy(ones_r[:, :], ones[:, :]).then_inc(ones_r_set, 1)

            def step(m, o):
                i = NJ * m + o
                if there(m, o, 3):
                    add_up(m, o - 3, 0)
                if there(m, o, 1):
                    dve.wait_ge(sq_summed, i)
                    dve.tensor_scalar(mean_sq[:, :], sq_ps[:, 0:TPC], 1.0 / H, RMS_EPS, op0=ALU.mult,
                                      op1=ALU.add).then_inc(mean_ready, 1)
                if there(m, o, 3):
                    add_up(m, o - 3, 1)
                square(m, o, range(0, 2))
                if there(m, o, 1):
                    dve.wait_ge(rms_ready, i)
                    wait(dve, r_spread, i - 1)
                    for t in range(TPC):
                        last = dve.tensor_scalar(diag[:, 0, t * P:(t + 1) * P], ident[:, :], rms_inv[:, t:t + 1], None,
                                                 op0=ALU.mult)
                    last.then_inc(diag_hi, 1)
                    dve.wait_ge(diag_hi, i)
                    for t in range(TPC):
                        cols = slice(t * P, (t + 1) * P)
                        last = dve.scalar_tensor_tensor(diag[:, 1, cols], ident[:, :], rms_inv[:, t:t + 1],
                                                        diag[:, 0, cols].bitcast(F32), op0=ALU.mult, op1=ALU.subtract)
                    last.then_inc(diag_ready, 1)
                if there(m, o, 3):
                    add_up(m, o - 3, 2)
                    add_up(m, o - 3, 3)
                square(m, o, range(2, 5))
                if there(m, o, 1):
                    for h in range(2):
                        scale(m, o - 1, h)
                square(m, o, range(5, HK))
                if there(m, o, 3):
                    dve.wait_ge(rstd2_ready, i - 2)
                    for t in range(TPC):
                        v = out[:, (o - 3) % 2, t, :]
                        dve.tensor_scalar(v, v, mv[:, t, 0:1], rstd2[:, t:t + 1], op0=ALU.subtract,
                                          op1=ALU.mult).then_inc(out_ready, 1)
                if there(m, o, 1):
                    for h in range(2, HK):
                        scale(m, o - 1, h)
                        split(m, o - 1, h - 2)
                    for h in (HK - 2, HK - 1):
                        split(m, o - 1, h)

            over_steps(dve, step)

        @block.tensor
        def _(pe):
            pe.wait_ge(ones_set, 3)
            pe.wait_ge(ones_r_set, 1)

            def sum_squares(m, o):
                i = NJ * m + o
                pe.wait_ge(sq_added, (i + 1) * (HK - 1))
                wait(pe, mean_ready, i)
                for t in range(TPC):
                    last = pe.matmul(sq_ps[:, t:t + 1], sum_sq[:, o % 2, t * P:(t + 1) * P], ones[:, 0:1],
                                     start=True, stop=True)
                last.then_inc(sq_summed, 1)

            def spread_rms(m, o):
                i = NJ * m + o
                pe.wait_ge(diag_ready, i + 1)
                wait(pe, z_ready, i * HK)
                pe.matmul(r_ps[:, :], ones_r[:, :], diag[:, 0, :], start=True, stop=False)
                pe.matmul(r_ps[:, :], ones_r[:, :], diag[:, 1, :], start=False, stop=True).then_inc(r_spread, 1)

            def step(m, o):
                i = NJ * m + o
                if there(m, o, 0):
                    pe.wait_ge(agg_here[o % 2], (used(m, o) + 1) * 16)
                    if isinstance(m, int) and m == 0 and o == 0:
                        pe.wait_ge(w_ready, 1)
                    a_hi = agg_in[:, o % 2, 0, :, :]
                    a_lo = agg_in[:, o % 2, 1, :, :]
                if there(m, o, 0):
                    for h in range(HK):
                        wait(pe, h_ready, i * HK + h - 1)
                        bank = h_ps[h % 2][:, :]
                        cols = slice(h * P, (h + 1) * P)
                        for k in range(DK):
                            pe.matmul(bank, w1s[:, 0, k, cols], a_hi[:, k, :], start=(k == 0), stop=False)
                            pe.matmul(bank, w1s[:, 0, k, cols], a_lo[:, k, :], start=False, stop=False)
                            last = pe.matmul(bank, w1s[:, 1, k, cols], a_hi[:, k, :], start=False, stop=(k == DK - 1))
                        last.then_inc(h_done, 1)
                        if there(m, o, 1) and h == 1:
                            sum_squares(m, o - 1)
                        if there(m, o, 1) and h == 5:
                            spread_rms(m, o - 1)
                if there(m, o, 1) and not there(m, o, 0):
                    sum_squares(m, o - 1)
                if there(m, o, 2):
                    banks = product_banks(m, o - 2)
                    if isinstance(m, int) and i == 2:
                        pe.wait_ge(w_ready, 2)
                    if banks is last_ps:
                        pe.wait_ge(h_ready, NC * HK)
                        pe.wait_ge(mean_ready, NC)
                        pe.wait_ge(z_ready, NC * HK)
                    for h in range(HK):
                        pe.wait_ge(slo_ready, (i - 2) * HK + h + 1)
                        for t in range(TPC):
                            if h == 0 and banks is o_ps:
                                wait(pe, o_read, (i - 3) * TPC + t + 1)
                            cols = slice(t * P, (t + 1) * P)
                            pe.matmul(banks[t][:, :], s_hi[:, h, cols], w2s[:, h, :, :].rearrange("p s d -> p (s d)"),
                                      start=(h == 0), stop=False)
                            last = pe.matmul(banks[t][:, 0:D], s_lo[:, h, cols], w2s[:, h, 0, :],
                                             start=False, stop=(h == HK - 1))
                        last.then_inc(w2_done, 1)
                        if h == TAIL_SPREAD and not there(m, o, 0) and there(m, o, 1):
                            spread_rms(m, o - 1)

            over_steps(pe, step)


_OUT = ((8, 2048, 256), "float32")


def kernel(x, adj, L0_gnn_weight, L0_gnn_bias, L1_gnn_epsilon, L1_gnn_W1, L1_gnn_b1, L1_gnn_rms_weight, L1_gnn_W2,
           L1_gnn_b2):
    import numpy as np
    import concourse.bacc as bacc
    from concourse.bass_utils import run_bass_kernel_spmd

    nc = bacc.Bacc("TRN2", target_bir_lowering=False, num_devices=1, dynamic_dma_scratch_size=1024)
    arrays = {
        "x": np.asarray(x),
        "adj": np.asarray(adj),
        "w0": np.asarray(L0_gnn_weight),
        "bias0": np.asarray(L0_gnn_bias).reshape(1, -1),
        "eps": np.asarray(L1_gnn_epsilon).reshape(1, 1),
        "w1": np.asarray(L1_gnn_W1),
        "b1": np.asarray(L1_gnn_b1),
        "rms_w": np.asarray(L1_gnn_rms_weight),
        "w2": np.asarray(L1_gnn_W2),
        "b2": np.asarray(L1_gnn_b2).reshape(1, -1),
    }
    args = {n: nc.dram_tensor(n, a.shape, mybir.dt.from_np(a.dtype), kind="ExternalInput").ap()
            for n, a in arrays.items()}
    y = nc.dram_tensor("y", _OUT[0], F32, kind="ExternalOutput").ap()
    build(nc, **args, y=y)
    results = run_bass_kernel_spmd(nc, [arrays], core_ids=[0]).results
    return results[0]["y"]
```
